# Optimizing a Trainium2 kernel written in Bass

```python
import numpy as np
import jax
import jax.numpy as jnp

def _softmax(x, axis=-1):
    return jax.nn.softmax(x, axis=axis)

def _gelu(x):
    return jax.nn.gelu(x, approximate=True)

def _silu(x):
    return jax.nn.silu(x)

def _sigmoid(x):
    return jax.nn.sigmoid(x)

def _layernorm(x, axis=-1, eps=1e-05):
    m = jnp.mean(x, axis=axis, keepdims=True)
    v = jnp.var(x, axis=axis, keepdims=True)
    return (x - m) / jnp.sqrt(v + eps)

def _scatter_add(tgt, idx, src, axis=0):
    return tgt.at[idx].add(src)

def _segment_sum(src, seg, n):
    return jax.ops.segment_sum(src, seg, n)
kernel_name = 'mk_gnn_preln_d2_gnn_r32_ae26cc'

def setup_inputs(seed: int=0):
    np.random.seed(seed)
    _w = jnp.asarray

    def _rec_inputs():
        import jax
        import jax.numpy as jnp
        _gk = jax.random.key(seed)
        x = -0.000202 + 1 * jax.random.normal(jax.random.fold_in(_gk, 1), (3125, 160), jnp.float32)
        _s = jax.random.randint(jax.random.fold_in(_gk, 2), (50000,), 0, 3125, jnp.int32)
        _d = jax.random.randint(jax.random.fold_in(_gk, 3), (50000,), 0, 3125, jnp.int32)
        _loop = jnp.arange(3125, dtype=jnp.int32)
        src = jnp.concatenate([_s, _d, _loop])
        dst = jnp.concatenate([_d, _s, _loop])
        _o = jnp.argsort(dst, stable=True)
        src = src[_o]
        dst = dst[_o]
        edge_attr_4 = 0.0012443 + 1.0001 * jax.random.normal(jax.random.fold_in(_gk, 12), (103125, 4), jnp.float32)
        edge_attr_64 = 0.000127647 + 1.00004 * jax.random.normal(jax.random.fold_in(_gk, 13), (103125, 64), jnp.float32)
        node_vec1 = jax.random.uniform(jax.random.fold_in(_gk, 15), (3125, 1), jnp.float32, 0.0, 1)
        return (x, src, dst, edge_attr_4, edge_attr_64, node_vec1)
    x, src, dst, edge_attr_4, edge_attr_64, node_vec1 = _rec_inputs()

    def _L0_gnn_setup():
        import jax, jax.numpy as jnp
        import numpy as np
        N, E = (1250, 20000)
        S_IN, V_IN = (64, 32)
        S_MID, V_MID = (96, 128)
        S_OUT, V_OUT = (96, 32)
        R = 64
        FC_HID = 64
        W_NUMEL = 64 + 64 + 32 + 32 + 32
        NUM_NEIGHBORS = 16.0

        def _inv(d):
            return 1.0 / jnp.sqrt(jnp.float32(d))

        def _forward(node_features, node_attr, edge_attr, edge_scalars, lin1_ws, lin1_wv, fc_w1, fc_w2, sc_ws, sc_wv, lin2_ws, lin2_wv, edge_src, edge_dst):
            n = node_features.shape[0]
            s = node_features[:, :S_IN]
            v = node_features[:, S_IN:].reshape(n, V_IN, 3)
            a = node_attr
            sc_s = s @ sc_ws * a * _inv(S_IN)
            sc_v = jnp.einsum('nci,cd->ndi', v, sc_wv) * a[:, :, None] * _inv(V_IN)
            h_s = s @ lin1_ws * a * _inv(S_IN)
            h_v = jnp.einsum('nci,cd->ndi', v, lin1_wv) * a[:, :, None] * _inv(V_IN)
            hid = jax.nn.silu(edge_scalars @ fc_w1 * _inv(R))
            w = hid @ fc_w2 * _inv(FC_HID)
            w1, w2, w3, w4, w5 = jnp.split(w, [64, 128, 160, 192], axis=-1)
            es = h_s[edge_src]
            ev = h_v[edge_src]
            e0 = edge_attr[:, :1]
            e1 = edge_attr[:, 1:4]
            m_s1 = w1 * es * e0
            m_s2 = w4 * jnp.einsum('eci,ei->ec', ev, e1) * _inv(3)
            m_v1 = (w2 * es)[:, :, None] * e1[:, None, :]
            m_v2 = w3[:, :, None] * ev * e0[:, :, None]
            m_v3 = w5[:, :, None] * jnp.cross(ev, e1[:, None, :]) * _inv(2)
            mid_s = jnp.concatenate([m_s1, m_s2], axis=-1)
            mid_v = jnp.concatenate([m_v1, m_v2, m_v3], axis=1)
            inv_nn = 1.0 / jnp.sqrt(jnp.float32(NUM_NEIGHBORS))
            agg_s = jax.ops.segment_sum(mid_s, edge_dst, num_segments=n) * inv_nn
            agg_v = jax.ops.segment_sum(mid_v, edge_dst, num_segments=n) * inv_nn
            o_s = agg_s @ lin2_ws * a * _inv(S_MID)
            o_v = jnp.einsum('nci,cd->ndi', agg_v, lin2_wv) * a[:, :, None] * _inv(V_MID)
            pre_s = sc_s + o_s
            pre_v = sc_v + o_v
            scalars = jax.nn.silu(pre_s[:, :64])
            gates = jax.nn.sigmoid(pre_s[:, 64:96])
            gated = gates[:, :, None] * pre_v
            return jnp.concatenate([scalars, gated.reshape(n, 3 * V_OUT)], axis=-1)
        key = jax.random.key(seed)
        ks = jax.random.split(key, 13)
        return {'node_features': jax.random.normal(ks[0], (N, S_IN + 3 * V_IN), jnp.float32), 'node_attr': jnp.ones((N, 1), jnp.float32), 'edge_src': jax.random.randint(ks[1], (E,), 0, N), 'edge_dst': jax.random.randint(ks[2], (E,), 0, N), 'edge_attr': jax.random.normal(ks[3], (E, 4), jnp.float32), 'edge_scalars': jax.random.normal(ks[4], (E, R), jnp.float32), 'lin1_ws': jax.random.normal(ks[5], (S_IN, S_IN), jnp.float32), 'lin1_wv': jax.random.normal(ks[6], (V_IN, V_IN), jnp.float32), 'fc_w1': jax.random.normal(ks[7], (R, FC_HID), jnp.float32), 'fc_w2': jax.random.normal(ks[8], (FC_HID, W_NUMEL), jnp.float32), 'sc_ws': jax.random.normal(ks[9], (S_IN, S_OUT), jnp.float32), 'sc_wv': jax.random.normal(ks[10], (V_IN, V_OUT), jnp.float32), 'lin2_ws': jax.random.normal(ks[11], (S_MID, S_OUT), jnp.float32), 'lin2_wv': jax.random.normal(ks[12], (V_MID, V_OUT), jnp.float32)}
    _L0_gnn_all = _L0_gnn_setup()
    _L0_gnn_in = {k: v for k, v in _L0_gnn_all.items() if k in ('lin1_ws', 'lin1_wv', 'fc_w1', 'fc_w2', 'sc_ws', 'sc_wv', 'lin2_ws', 'lin2_wv')}
    del _L0_gnn_all

    def _L1_gnn_setup():
        import jax, jax.numpy as jnp
        import numpy as np
        N, E = (50000, 25000)
        MUL0, MUL1 = (64, 32)
        D = MUL0 + 3 * MUL1
        INV3 = float(1.0 / np.sqrt(3.0))
        INV6 = float(1.0 / np.sqrt(6.0))
        C0 = float(1.0 / np.sqrt(MUL0 + MUL1))
        C1 = float(np.sqrt(3.0 / (MUL0 + 2 * MUL1)))
        LIN_S = float(1.0 / np.sqrt(MUL0))
        LIN_V = float(1.0 / np.sqrt(MUL1))
        key = jax.random.key(seed)
        ks = jax.random.split(key, 10)
        x = jax.random.normal(ks[0], (N, D), dtype=jnp.float32)
        sh = jax.random.normal(ks[1], (E, 4), dtype=jnp.float32)
        edge_index = jax.random.randint(ks[2], (2, E), 0, N, dtype=jnp.int64)
        W1 = jax.random.normal(ks[3], (MUL0, MUL0), dtype=jnp.float32)
        W2 = jax.random.normal(ks[4], (MUL1, MUL0), dtype=jnp.float32)
        W3 = jax.random.normal(ks[5], (MUL0, MUL1), dtype=jnp.float32)
        W4 = jax.random.normal(ks[6], (MUL1, MUL1), dtype=jnp.float32)
        W5 = jax.random.normal(ks[7], (MUL1, MUL1), dtype=jnp.float32)
        Ws = jax.random.normal(ks[8], (MUL0, MUL0), dtype=jnp.float32)
        Wv = jax.random.normal(ks[9], (MUL1, MUL1), dtype=jnp.float32)
        return {'x': x, 'sh': sh, 'W1': W1, 'W2': W2, 'W3': W3, 'W4': W4, 'W5': W5, 'Ws': Ws, 'Wv': Wv, 'edge_index': edge_index}
    _L1_gnn_all = _L1_gnn_setup()
    _L1_gnn_in = {k: v for k, v in _L1_gnn_all.items() if k in ('W1', 'W2', 'W3', 'W4', 'W5', 'Ws', 'Wv')}
    del _L1_gnn_all
    return {'x': x, 'src': src, 'dst': dst, 'edge_attr_4': edge_attr_4, 'edge_attr_64': edge_attr_64, 'node_vec1': node_vec1, 'L0_gnn_lin1_ws': _L0_gnn_in['lin1_ws'], 'L0_gnn_lin1_wv': _L0_gnn_in['lin1_wv'], 'L0_gnn_fc_w1': _L0_gnn_in['fc_w1'], 'L0_gnn_fc_w2': _L0_gnn_in['fc_w2'], 'L0_gnn_sc_ws': _L0_gnn_in['sc_ws'], 'L0_gnn_sc_wv': _L0_gnn_in['sc_wv'], 'L0_gnn_lin2_ws': _L0_gnn_in['lin2_ws'], 'L0_gnn_lin2_wv': _L0_gnn_in['lin2_wv'], 'L1_gnn_W1': _L1_gnn_in['W1'], 'L1_gnn_W2': _L1_gnn_in['W2'], 'L1_gnn_W3': _L1_gnn_in['W3'], 'L1_gnn_W4': _L1_gnn_in['W4'], 'L1_gnn_W5': _L1_gnn_in['W5'], 'L1_gnn_Ws': _L1_gnn_in['Ws'], 'L1_gnn_Wv': _L1_gnn_in['Wv']}

def reference(x, src, dst, edge_attr_4, edge_attr_64, node_vec1, L0_gnn_lin1_ws, L0_gnn_lin1_wv, L0_gnn_fc_w1, L0_gnn_fc_w2, L0_gnn_sc_ws, L0_gnn_sc_wv, L0_gnn_lin2_ws, L0_gnn_lin2_wv, L1_gnn_W1, L1_gnn_W2, L1_gnn_W3, L1_gnn_W4, L1_gnn_W5, L1_gnn_Ws, L1_gnn_Wv):
    import jax
    import jax.numpy as jnp

    def _L0_gnn_ref(node_features, node_attr, edge_src, edge_dst, edge_attr, edge_scalars, lin1_ws, lin1_wv, fc_w1, fc_w2, sc_ws, sc_wv, lin2_ws, lin2_wv):
        import jax, jax.numpy as jnp
        import numpy as np
        N, E = (1250, 20000)
        S_IN, V_IN = (64, 32)
        S_MID, V_MID = (96, 128)
        S_OUT, V_OUT = (96, 32)
        R = 64
        FC_HID = 64
        W_NUMEL = 64 + 64 + 32 + 32 + 32
        NUM_NEIGHBORS = 16.0

        def _inv(d):
            return 1.0 / jnp.sqrt(jnp.float32(d))

        def _forward(node_features, node_attr, edge_attr, edge_scalars, lin1_ws, lin1_wv, fc_w1, fc_w2, sc_ws, sc_wv, lin2_ws, lin2_wv, edge_src, edge_dst):
            n = node_features.shape[0]
            s = node_features[:, :S_IN]
            v = node_features[:, S_IN:].reshape(n, V_IN, 3)
            a = node_attr
            sc_s = s @ sc_ws * a * _inv(S_IN)
            sc_v = jnp.einsum('nci,cd->ndi', v, sc_wv) * a[:, :, None] * _inv(V_IN)
            h_s = s @ lin1_ws * a * _inv(S_IN)
            h_v = jnp.einsum('nci,cd->ndi', v, lin1_wv) * a[:, :, None] * _inv(V_IN)
            hid = jax.nn.silu(edge_scalars @ fc_w1 * _inv(R))
            w = hid @ fc_w2 * _inv(FC_HID)
            w1, w2, w3, w4, w5 = jnp.split(w, [64, 128, 160, 192], axis=-1)
            es = h_s[edge_src]
            ev = h_v[edge_src]
            e0 = edge_attr[:, :1]
            e1 = edge_attr[:, 1:4]
            m_s1 = w1 * es * e0
            m_s2 = w4 * jnp.einsum('eci,ei->ec', ev, e1) * _inv(3)
            m_v1 = (w2 * es)[:, :, None] * e1[:, None, :]
            m_v2 = w3[:, :, None] * ev * e0[:, :, None]
            m_v3 = w5[:, :, None] * jnp.cross(ev, e1[:, None, :]) * _inv(2)
            mid_s = jnp.concatenate([m_s1, m_s2], axis=-1)
            mid_v = jnp.concatenate([m_v1, m_v2, m_v3], axis=1)
            inv_nn = 1.0 / jnp.sqrt(jnp.float32(NUM_NEIGHBORS))
            agg_s = jax.ops.segment_sum(mid_s, edge_dst, num_segments=n) * inv_nn
            agg_v = jax.ops.segment_sum(mid_v, edge_dst, num_segments=n) * inv_nn
            o_s = agg_s @ lin2_ws * a * _inv(S_MID)
            o_v = jnp.einsum('nci,cd->ndi', agg_v, lin2_wv) * a[:, :, None] * _inv(V_MID)
            pre_s = sc_s + o_s
            pre_v = sc_v + o_v
            scalars = jax.nn.silu(pre_s[:, :64])
            gates = jax.nn.sigmoid(pre_s[:, 64:96])
            gated = gates[:, :, None] * pre_v
            return jnp.concatenate([scalars, gated.reshape(n, 3 * V_OUT)], axis=-1)
        return _forward(node_features, node_attr, edge_attr, edge_scalars, lin1_ws, lin1_wv, fc_w1, fc_w2, sc_ws, sc_wv, lin2_ws, lin2_wv, edge_src, edge_dst)

    def _L1_gnn_ref(x, sh, W1, W2, W3, W4, W5, Ws, Wv, edge_index):
        import jax, jax.numpy as jnp
        import numpy as np
        N, E = (50000, 25000)
        MUL0, MUL1 = (64, 32)
        D = MUL0 + 3 * MUL1
        INV3 = float(1.0 / np.sqrt(3.0))
        INV6 = float(1.0 / np.sqrt(6.0))
        C0 = float(1.0 / np.sqrt(MUL0 + MUL1))
        C1 = float(np.sqrt(3.0 / (MUL0 + 2 * MUL1)))
        LIN_S = float(1.0 / np.sqrt(MUL0))
        LIN_V = float(1.0 / np.sqrt(MUL1))
        n = x.shape[0]
        src, dst = (edge_index[0], edge_index[1])
        s = x[:, :MUL0]
        v = x[:, MUL0:].reshape(n, MUL1, 3)
        ss, vv = (s[src], v[src])
        e0 = sh[:, 0:1]
        e1 = sh[:, 1:4]
        dot = jnp.einsum('eui,ei->eu', vv, e1)
        out0 = C0 * (ss * e0 @ W1 + dot * INV3 @ W2)
        p3 = (ss @ W3)[:, :, None] * e1[:, None, :] * INV3
        p4 = jnp.einsum('eui,uw->ewi', vv * e0[:, :, None], W4) * INV3
        p5 = jnp.einsum('eui,uw->ewi', jnp.cross(vv, e1[:, None, :]), W5) * INV6
        out1 = C1 * (p3 + p4 + p5)
        m = jnp.concatenate([out0, out1.reshape(-1, 3 * MUL1)], axis=1)
        m_agg = jax.ops.segment_sum(m, dst, num_segments=n)
        hs = m_agg[:, :MUL0] @ Ws * LIN_S
        hv = jnp.einsum('nui,uw->nwi', m_agg[:, MUL0:].reshape(n, MUL1, 3), Wv) * LIN_V
        h = jnp.concatenate([hs, hv.reshape(n, 3 * MUL1)], axis=1)
        return x + jax.nn.relu(h)
    edge_index = jnp.stack([src, dst])
    h = jnp.maximum(_layernorm(x, axis=-1), 0.0)
    x = x + _L0_gnn_ref(h, node_vec1, src, dst, edge_attr_4, edge_attr_64, L0_gnn_lin1_ws, L0_gnn_lin1_wv, L0_gnn_fc_w1, L0_gnn_fc_w2, L0_gnn_sc_ws, L0_gnn_sc_wv, L0_gnn_lin2_ws, L0_gnn_lin2_wv)
    h = jnp.maximum(_layernorm(x, axis=-1), 0.0)
    x = x + _L1_gnn_ref(h, edge_attr_4, L1_gnn_W1, L1_gnn_W2, L1_gnn_W3, L1_gnn_W4, L1_gnn_W5, L1_gnn_Ws, L1_gnn_Wv, edge_index)
    return x

_drawn_inputs = setup_inputs


def setup_inputs(seed=0):
    import zlib

    import numpy as np

    out = dict(_drawn_inputs(seed))
    spreads = {}
    factors = {}
    for name, (base, spread) in spreads.items():
        noise = np.random.default_rng([zlib.crc32(name.encode()), seed]).standard_normal(out[name].shape)
        drawn = base * np.exp(spread * noise) if base else spread * noise
        out[name] = jnp.asarray(drawn.astype(out[name].dtype))
    for name, factor in factors.items():
        out[name] = (out[name] * factor).astype(out[name].dtype)
    return out
```

```python
import numpy as np
from contextlib import ExitStack

import concourse.bass as bass
from concourse import mybir

F32 = mybir.dt.float32
I32 = mybir.dt.int32
ALU = mybir.AluOpType
ACT = mybir.ActivationFunctionType
AXX = mybir.AxisListType.X
RMAX = bass.bass_isa.ReduceOp.max

P = 128
N = 3125
E = 103125
NT = -(-N // P)
NPAD = NT * P
S_CH, V_CH = 64, 32
VC = 3 * V_CH
D = S_CH + VC
W_N = 2 * S_CH + 3 * V_CH
S_OUT = 96
PRE = S_OUT + VC
MSG = 2 * S_CH + 3 * VC
TILES = 4
GROUP = TILES * P
UNROLL = 4
GROUPS = -(-E // (GROUP * UNROLL)) * UNROLL
ITERS = GROUPS // UNROLL
E_PAD = GROUPS * GROUP
WIN = 32
ACC_W = NPAD + WIN
PLANES = 8
EPS = 1e-5

C_W1, C_W3, C_W4, C_W5, C_W2 = 0, S_CH, S_CH + VC, S_CH + 2 * VC, S_CH + 3 * VC
LOW = (0, P)
HIGH = (C_W4, MSG - P)


def build(nc, x, node_vec, src_idx, dst_idx, edge_sh, edge_feat, ident, iota, lin_sc, lin_sc_scale,
          fc1, fc2, big0, big0_scale, l1_pair, l1_pair_scale, l1_out, l1_out_scale, out):
    table = [nc.dram_tensor(f"node_table_{l}", (NPAD, D), F32, kind="Internal").ap() for l in range(2)]
    big1_kept = nc.dram_tensor("big1_kept", (P, PLANES, D), F32, kind="Internal").ap()
    x_v = x.rearrange("(n p) c -> p n c", p=P)
    out_v = out.rearrange("(n p) c -> p n c", p=P)
    table_v = [t.rearrange("(n p) c -> p n c", p=P) for t in table]

    ctx = ExitStack()
    with ctx:
        def sb(name, shape, dt=F32, scope=ctx):
            return scope.enter_context(nc.sbuf_tensor(name, shape, dt))

        def sem(name):
            return ctx.enter_context(nc.semaphore(name))

        acc = sb("acc", [P, PLANES, ACC_W])
        X = sb("X", [P, NT, D])
        sc = sb("sc", [P, NT, PRE])
        a_col = sb("a_col", [P, NT])
        dst = sb("dst", [P, GROUPS * TILES], I32)
        rel = sb("rel", [P, GROUPS * TILES])
        sh = sb("sh", [P, GROUPS * TILES, 4])
        first = sb("first", [P, GROUPS])
        place = sb("place", [1, GROUPS])
        place_i = sb("place_i", [1, GROUPS], I32)
        turns_f = sb("turns_f", [1, 1])
        turns_i = sb("turns_i", [1, 3], I32)
        ident_sb = sb("ident_sb", [P, P])
        iota_sb = sb("iota_sb", [P, WIN])
        fc1_sb = sb("fc1_sb", [P, P])
        fc2_sb = sb("fc2_sb", [P, 2 * W_N])
        big0_sb = sb("big0_sb", [P, PLANES, PRE])
        mean = sb("mean", [P, NT])
        var = sb("var", [P, NT])
        rstd = sb("rstd", [P, NT])
        eps_col = sb("eps_col", [P, 1])

        SQ = sc[:].rearrange("p n c -> p (n c)")[:, 0:NT * D].rearrange("p (n c) -> p n c", c=D)

        def layer_norm(name, H, ready, before):
            step = sem(name + "_dve_step")
            var_ready = sem(name + "_var_ready")
            root_ready = sem(name + "_root_ready")
            wide = [P, NT, D]

            def on_vector(dve):
                n = [0]

                def then(ins):
                    n[0] += 1
                    ins.then_inc(step, 1)
                    dve.wait_ge(step, n[0])

                before(dve)
                then(nc.vector.tensor_reduce(mean[:], X[:], AXX, ALU.add))
                then(nc.vector.tensor_scalar(mean[:], mean[:], 1.0 / D, None, ALU.mult))
                then(nc.vector.tensor_tensor(H[:], X[:], mean[:].unsqueeze(2).to_broadcast(wide), ALU.subtract))
                then(nc.vector.tensor_tensor(SQ, H[:], H[:], ALU.mult))
                then(nc.vector.tensor_reduce(var[:], SQ, AXX, ALU.add))
                nc.vector.tensor_scalar(var[:], var[:], 1.0 / D, None, ALU.mult).then_inc(var_ready, 1)
                dve.wait_ge(root_ready, 1)
                then(nc.vector.reciprocal(rstd[:], rstd[:]))
                then(nc.vector.tensor_tensor(H[:], H[:], rstd[:].unsqueeze(2).to_broadcast(wide), ALU.mult))
                nc.vector.tensor_scalar(H[:], H[:], 0.0, None, ALU.max).then_inc(ready, 1)

            def on_scalar(act):
                act.wait_ge(var_ready, 1)
                nc.scalar.activation(rstd[:], var[:], ACT.Sqrt, bias=eps_col[:, 0:1]).then_inc(root_ready, 1)

            return on_vector, on_scalar

        def windows(then):
            wide = [P, GROUPS, TILES]
            then(nc.vector.tensor_tensor(rel[:].rearrange("p (g t) -> p g t", t=TILES),
                                         dst[:].rearrange("p (g t) -> p g t", t=TILES),
                                         first[:].unsqueeze(2).to_broadcast(wide), ALU.subtract))
            then(nc.vector.tensor_copy(place[:], first[0:1, :]))
            then(nc.vector.tensor_copy(place_i[:], place[:]))

        with ExitStack() as st:
            H = sb("h0", [P, NT, D], scope=st)
            hT = sb("hT", [P, 2, 2, P], scope=st)
            rows = sb("rows", [P, 2, D], scope=st)
            big1 = sb("big1", [P, PLANES, D], scope=st)
            lin = acc[:, 0, 0:2 * (D + PRE)].rearrange("p (c n) -> p c n", c=2)
            lin_k = acc[:, 1, 0:2 * (D + PRE)].rearrange("p (c n) -> p c n", c=2)
            big_k = acc[:, 2, 0:PLANES * PRE].rearrange("p (c n) -> p c n", c=PLANES)
            pair = acc[:, 3:5, :].rearrange("p a n -> p (a n)")[:, 0:PLANES * 2 * P].rearrange("p (m n) -> p m n", n=P)
            pair_k = acc[:, 5:7, :].rearrange("p a n -> p (a n)")[:, 0:PLANES * 2 * P].rearrange("p (m n) -> p m n", n=P)
            wout = acc[:, 7, 0:2 * D].rearrange("p (c n) -> p c n", c=2)
            wout_k = acc[:, 7, 2 * D:4 * D].rearrange("p (c n) -> p c n", c=2)
            least = sb("least", [P, 2, GROUPS], scope=st)
            both = sb("both", [P, 2, GROUPS], scope=st)
            span = sb("span", [P, GROUPS], scope=st)
            tp = st.enter_context(nc.psum_tensor("tp", [P, 2, 2, 256], F32))
            mm = st.enter_context(nc.psum_tensor("mm", [P, 2, 512], F32))
            cp = st.enter_context(nc.psum_tensor("cp", [P, 2, 512], F32))

            x_in = sem("x_in")
            dst_in = sem("dst_in")
            w_in = sem("w_in")
            edges_in = sem("edges_in")
            h0_ready = sem("h0_ready")
            eps_set = sem("eps_set")
            least_ready = sem("least_ready")
            both_ready = sem("both_ready")
            weights_ready = sem("weights_ready")
            hT_turned = sem("hT_turned")
            hT_ready = sem("hT_ready")
            lin_done = sem("lin_done")
            rows_ready = sem("rows_ready")
            sc_ready = sem("sc_ready")
            rows_out = [sem(f"rows_out{i}") for i in range(2)]
            comp_done = sem("comp_done")
            comp_out = sem("comp_out")
            big1_out = sem("big1_out")
            acc_clear = sem("acc_clear")
            setup_step = sem("setup_step")
            norm_vector, norm_scalar = layer_norm("ln0", H, h0_ready, lambda e: e.wait_ge(x_in, 16))

            with nc.Block() as block:
                @block.sync
                def _(sp):
                    sp.dma_start(X[:], x_v).then_inc(x_in, 16)
                    sp.dma_start(dst[:], dst_idx).then_inc(dst_in, 16)
                    sp.dma_start(lin, lin_sc).then_inc(w_in, 16)
                    sp.dma_start(lin_k, lin_sc_scale).then_inc(w_in, 16)
                    sp.dma_start(ident_sb[:], ident).then_inc(w_in, 16)
                    sp.dma_start(iota_sb[:], iota).then_inc(w_in, 16)
                    sp.dma_start(a_col[:], node_vec).then_inc(w_in, 16)
                    sp.dma_start(big0_sb[:], big0).then_inc(w_in, 16)
                    sp.dma_start(big_k, big0_scale).then_inc(w_in, 16)
                    sp.dma_start(pair, l1_pair).then_inc(w_in, 16)
                    sp.dma_start(pair_k, l1_pair_scale).then_inc(w_in, 16)
                    sp.dma_start(wout, l1_out).then_inc(w_in, 16)
                    sp.dma_start(wout_k, l1_out_scale).then_inc(w_in, 16)
                    sp.dma_start(fc1_sb[:], fc1).then_inc(edges_in, 16)
                    sp.dma_start(fc2_sb[:], fc2).then_inc(edges_in, 16)
                    sp.dma_start(sh[:], edge_sh).then_inc(edges_in, 16)
                    for n in range(NT):
                        sp.wait_ge(rows_ready, n + 1)
                        sp.dma_start(table_v[0][:, n, :], rows[:, n % 2, :]).then_inc(rows_out[n % 2], 16)
                    sp.wait_ge(rows_out[0], 16 * ((NT + 1) // 2))
                    sp.wait_ge(rows_out[1], 16 * (NT // 2))
                    sp.wait_ge(comp_out, 1)
                    sp.dma_start(big1_kept, big1[:]).then_inc(big1_out, 16)
                    sp.wait_ge(big1_out, 16)
                    sp.wait_ge(edges_in, 48)

                @block.gpsimd
                def _(pool):
                    pool.wait_ge(least_ready, 1)
                    nc.gpsimd.partition_all_reduce(both[:].rearrange("p a g -> p (a g)"),
                                                   least[:].rearrange("p a g -> p (a g)"), P, RMAX).then_inc(both_ready, 1)
                    pool.wait_ge(comp_out, 1)
                    pool.wait_ge(lin_done, NT)
                    nc.gpsimd.memset(acc[:], 0.0).then_inc(acc_clear, 1)
                    pool.wait_ge(acc_clear, 1)

                @block.vector
                def _(dve):
                    n = [0]

                    def then(ins):
                        n[0] += 1
                        ins.then_inc(setup_step, 1)
                        dve.wait_ge(setup_step, n[0])

                    nc.vector.memset(eps_col[:], EPS).then_inc(eps_set, 1)
                    norm_vector(dve)
                    dve.wait_ge(w_in, 11 * 16)
                    then(nc.vector.tensor_tensor(lin, lin, lin_k, ALU.mult))
                    then(nc.vector.tensor_tensor(pair, pair, pair_k, ALU.mult))
                    then(nc.vector.tensor_tensor(wout, wout, wout_k, ALU.mult))
                    nc.vector.tensor_tensor(big0_sb[:], big0_sb[:], big_k, ALU.mult).then_inc(weights_ready, 1)
                    dve.wait_ge(dst_in, 16)
                    by_group = dst[:].rearrange("p (g t) -> p g t", t=TILES)
                    then(nc.vector.tensor_reduce(least[:, 0, :], by_group, AXX, ALU.min))
                    then(nc.vector.tensor_scalar(least[:, 0, :], least[:, 0, :], -1.0, None, ALU.mult))
                    nc.vector.tensor_reduce(least[:, 1, :], by_group, AXX, ALU.max).then_inc(least_ready, 1)
                    for t in range(NT):
                        dve.wait_ge(lin_done, t + 1)
                        if t >= 2:
                            dve.wait_ge(rows_out[t % 2], 16 * (t // 2))
                        nc.vector.tensor_scalar(rows[:, t % 2, :], mm[:, t % 2, 0:D], a_col[:, t:t + 1],
                                                None, ALU.mult).then_inc(rows_ready, 1)
                        nc.vector.tensor_copy(sc[:, t, :], mm[:, t % 2, D:D + PRE]).then_inc(sc_ready, 1)
                    dve.wait_ge(both_ready, 1)
                    then(nc.vector.tensor_scalar(first[:], both[:, 0, :], -1.0, None, ALU.mult))
                    then(nc.vector.tensor_tensor(span[:], both[:, 0, :], both[:, 1, :], ALU.add))
                    then(nc.vector.tensor_reduce(turns_f[:], span[0:1, :], AXX, ALU.max))
                    then(nc.vector.tensor_copy(turns_i[:, 0:1], turns_f[:]))
                    then(nc.vector.tensor_scalar(turns_i[:, 1:2], turns_i[:, 0:1], WIN.bit_length() - 1, None,
                                                 ALU.arith_shift_right))
                    then(nc.vector.tensor_scalar(turns_i[:, 2:3], turns_i[:, 1:2], float(ITERS), float(ITERS),
                                                 ALU.mult, ALU.add))
                    windows(then)

                @block.scalar
                def _(act):
                    act.wait_ge(eps_set, 1)
                    norm_scalar(act)
                    for t in range(NT):
                        act.wait_ge(hT_turned, t + 1)
                        if t >= 2:
                            act.wait_ge(lin_done, t - 1)
                        nc.scalar.activation(hT[:, t % 2, :, :], tp[:, t % 2, :, 0:P], ACT.Copy).then_inc(hT_ready, 1)
                    for m in range(PLANES // 2):
                        act.wait_ge(comp_done, m + 1)
                        last = nc.scalar.activation(big1[:, 2 * m:2 * m + 2, :],
                                                    cp[:, m % 2, 0:2 * D].rearrange("p (c n) -> p c n", c=2), ACT.Copy)
                        last.then_inc(comp_out if m == PLANES // 2 - 1 else hT_ready, 1)

                @block.tensor
                def _(pe):
                    pe.wait_ge(weights_ready, 1)
                    pe.wait_ge(h0_ready, 1)
                    for t in range(NT + 1):
                        if t < NT:
                            if t >= 2:
                                pe.wait_ge(hT_ready, t - 1)
                            nc.tensor.transpose(tp[:, t % 2, 0, 0:P], H[:, t, 0:P], ident_sb[:])
                            nc.tensor.transpose(tp[:, t % 2, 1, 0:P], H[:, t, D - P:D], ident_sb[:]).then_inc(hT_turned, 1)
                        if t >= 1:
                            u = t - 1
                            pe.wait_ge(hT_ready, u + 1)
                            if u >= 2:
                                pe.wait_ge(rows_ready, u - 1)
                                pe.wait_ge(sc_ready, u - 1)
                            for c in range(2):
                                last = nc.tensor.matmul(mm[:, u % 2, 0:D + PRE], hT[:, u % 2, c, :], lin[:, c, :],
                                                        start=(c == 0), stop=(c == 1))
                            last.then_inc(lin_done, 1)
                    for m in range(PLANES // 2):
                        if m >= 2:
                            pe.wait_ge(hT_ready, NT + m - 1)
                        for h in range(2):
                            for c in range(2):
                                last = nc.tensor.matmul(cp[:, m % 2, h * D:(h + 1) * D], pair[:, 2 * (2 * m + h) + c, :],
                                                        wout[:, c, :], start=(c == 0), stop=(c == 1))
                        last.then_inc(comp_done, 1)

        def edge_passes(layer):
            L = f"l{layer}_"
            own_weights = layer == 0
            width = MSG if own_weights else D
            chunks = 4 if own_weights else 2
            with ExitStack() as st:
                idx = sb(L + "idx", [P, 2, 2 * TILES], I32, scope=st)
                g = sb(L + "g", [P, UNROLL, TILES, D], scope=st)
                hot = sb(L + "hot", [P, 2, TILES, WIN], scope=st)
                sel = sb(L + "sel", [P, 2, TILES, 4 * WIN], scope=st)
                sums_sb = sb(L + "sums_sb", [P, 2, width], scope=st)
                sums = st.enter_context(nc.psum_tensor(L + "sums", [P, 2, 512], F32))
                turned = st.enter_context(nc.psum_tensor(L + "turned", [P, 2, 4, P], F32))
                if own_weights:
                    feat = sb(L + "feat", [P, UNROLL, GROUP // 2], scope=st)
                    hid = sb(L + "hid", [P, 2, GROUP // 2], scope=st)
                    prod = sb(L + "prod", [P, 2, TILES, MSG], scope=st)
                    hid_ps = st.enter_context(nc.psum_tensor(L + "hid_ps", [P, 2, 512], F32))
                    w_ps = st.enter_context(nc.psum_tensor(L + "w_ps", [P, 2, 512], F32))

                idx_in = [sem(L + f"idx_in{h}") for h in range(2)]
                feat_in = [sem(L + f"feat_in{u}") for u in range(UNROLL)]
                gathered = [sem(L + f"gathered{u}") for u in range(UNROLL)]
                hid_done = sem(L + "hid_done")
                silu_done = sem(L + "silu_done")
                w_done = sem(L + "w_done")
                prod_done = sem(L + "prod_done")
                hot_done = sem(L + "hot_done")
                sel_done = sem(L + "sel_done")
                agg_done = sem(L + "agg_done")
                sums_copied = sem(L + "sums_copied")
                turn_done = sem(L + "turn_done")
                acc_done = sem(L + "acc_done")
                gather_begun = sem(L + "gather_begun")
                pass_left = sem(L + "pass_left")

                def passes(eng):
                    total = eng.value_load(turns_i[0:1, 2:3], min_val=ITERS, max_val=ITERS * (-(-N // WIN)))
                    return eng.Fori(0, total, ITERS)

                def pass_over(eng, q):
                    end = eng.snap(UNROLL * q + GROUPS)
                    eng.wait_ge(acc_done, end)
                    eng.sem_inc(pass_left, 1)

                def stages(eng, q, stage, last):
                    for s in range(UNROLL):
                        stage(q, 0, s, s)
                    with eng.Fori(1, ITERS - 1) as it:
                        f = eng.snap(q + it)
                        for o in range(UNROLL):
                            stage(f, it, o, None)
                    f = eng.snap(q + (ITERS - 1))
                    for s in range(GROUPS - UNROLL, last):
                        stage(f, ITERS - 1, s - (GROUPS - UNROLL), s)

                with nc.Block() as block:
                    @block.sync
                    def _(sp):
                        def load_idx(pair, h):
                            sp.dma_start(idx[:, h, :], src_idx[bass.ds(pair, 1), :, :].rearrange("a p t -> (a p) t")).then_inc(idx_in[h], 16)

                        def load_feat(group, u):
                            sp.dma_start(feat[:, u, :], edge_feat[bass.ds(group, 1), :, :].rearrange("a p c -> (a p) c")).then_inc(feat_in[u], 16)

                        with passes(sp) as q:
                            for h in range(2):
                                load_idx(h, h)
                            if own_weights:
                                for u in range(UNROLL):
                                    load_feat(u, u)
                            with sp.Fori(0, ITERS - 1) as it:
                                f = sp.snap(q + it)
                                for u in range(UNROLL):
                                    group = sp.snap(UNROLL * it + (UNROLL + u))
                                    if u % 2:
                                        pair = sp.snap(2 * it + (2 + u // 2))
                                        rows = sp.snap(16 * TILES * f + 16 * TILES)
                                        sp.wait_ge(gathered[u - 1], rows)
                                        sp.wait_ge(gathered[u], rows)
                                        load_idx(pair, u // 2)
                                    if own_weights:
                                        used = sp.snap(UNROLL * f + (u + 1))
                                        sp.wait_ge(hid_done, used)
                                        load_feat(group, u)
                            pass_over(sp, q)

                    @block.gpsimd
                    def _(pool):
                        def gather(f, u, full):
                            used = pool.snap(2 * UNROLL * f + (2 * u + 2 - 2 * UNROLL)) if full else None
                            there = pool.snap(16 * f + 16)
                            if u % 2 == 0:
                                pool.wait_ge(idx_in[u // 2], there)
                            if full:
                                pool.wait_ge(prod_done if own_weights else agg_done, used)
                            if full or u % 2 == 0:
                                pool.sem_inc(gather_begun, 1)
                            for j in range(TILES):
                                nc.gpsimd.indirect_dma_start(
                                    out=g[:, u, j, :], out_offset=None, in_=table[layer],
                                    in_offset=bass.IndirectOffsetOnAxis(ap=idx[:, u // 2, (u % 2) * TILES + j:(u % 2) * TILES + j + 1], axis=0),
                                ).then_inc(gathered[u], 16)

                        with passes(pool) as q:
                            for u in range(UNROLL):
                                gather(q, u, False)
                            with pool.Fori(1, ITERS) as it:
                                f = pool.snap(q + it)
                                for u in range(UNROLL):
                                    gather(f, u, True)
                            pass_over(pool, q)

                    @block.scalar
                    def _(act):
                        def silu(f, o, s):
                            act.wait_ge(hid_done, UNROLL * f + (o + 1))
                            if s is None or s >= 2:
                                act.wait_ge(w_done, 2 * UNROLL * f + (2 * o - 2))
                            nc.scalar.activation(hid[:, o % 2, :], hid_ps[:, o % 2, 0:GROUP // 2], ACT.Silu,
                                                 scale=float(S_CH) ** -0.5).then_inc(silu_done, 1)

                        def copy_sums(f, o, s):
                            act.wait_ge(agg_done, 2 * UNROLL * f + (2 * o + 2))
                            if s is None or s >= 2:
                                act.wait_ge(turn_done, UNROLL * f + (o - 1))
                            nc.scalar.activation(sums_sb[:, o % 2, :], sums[:, o % 2, 0:width], ACT.Copy).then_inc(sums_copied, 1)

                        def stage(f, it, o, s):
                            if own_weights:
                                if s == 0:
                                    silu(f, 0, 0)
                                if s is None or s >= 2:
                                    copy_sums(f, o - 2, None if s is None else s - 2)
                                if s is None or s + 1 < GROUPS:
                                    silu(f, o + 1, None if s is None else s + 1)
                            else:
                                copy_sums(f, o, s)

                        with passes(act) as q:
                            stages(act, q, stage, GROUPS + 2 if own_weights else GROUPS)
                            pass_over(act, q)

                    @block.vector
                    def _(dve):
                        def select(f, it, o, s):
                            if s is None or s >= 2:
                                dve.wait_ge(agg_done, 2 * UNROLL * f + (2 * o - 2))
                            at = bass.ds(UNROLL * TILES * it + TILES * o, TILES)
                            nc.vector.tensor_tensor(hot[:, o % 2, :, :], iota_sb[:].unsqueeze(1).to_broadcast([P, TILES, WIN]),
                                                    rel[:, at].unsqueeze(2).to_broadcast([P, TILES, WIN]),
                                                    ALU.is_equal).then_inc(hot_done, 1)
                            dve.wait_ge(hot_done, UNROLL * f + (o + 1))
                            nc.vector.tensor_tensor(sel[:, o % 2, :, :].rearrange("p t (k n) -> p t k n", k=4),
                                                    hot[:, o % 2, :, :].unsqueeze(2).to_broadcast([P, TILES, 4, WIN]),
                                                    sh[:, at, :].unsqueeze(3).to_broadcast([P, TILES, 4, WIN]),
                                                    ALU.mult).then_inc(sel_done, 1)

                        def products(f, o, h):
                            u = o % UNROLL
                            dve.wait_ge(w_done, 2 * UNROLL * f + (2 * o + h + 1))
                            if h == 0:
                                dve.wait_ge(gathered[u], 16 * TILES * f + 16 * TILES * (o // UNROLL + 1))
                            w = w_ps[:, h, 0:2 * W_N].rearrange("p (t c) -> p t c", t=2)
                            rows = g[:, u, 2 * h:2 * h + 2, :]
                            to = prod[:, o % 2, 2 * h:2 * h + 2, :]
                            s_cols = to[:, :, 0:S_CH]
                            both = bass.AP(s_cols.tensor, s_cols.offset,
                                           [*s_cols.ap[0:2], [C_W2 - C_W1, 2], s_cols.ap[2]])
                            for t in range(2):
                                nc.vector.tensor_tensor(
                                    to[:, t, C_W3:C_W2].rearrange("p (j c i) -> p j c i", j=3, i=3),
                                    w[:, t, 2 * S_CH:W_N].rearrange("p (j c) -> p j c", j=3).unsqueeze(3).to_broadcast([P, 3, V_CH, 3]),
                                    rows[:, t, S_CH:D].rearrange("p (c i) -> p c i", i=3).unsqueeze(1).to_broadcast([P, 3, V_CH, 3]),
                                    ALU.mult)
                            nc.vector.tensor_tensor(
                                both,
                                w[:, :, 0:2 * S_CH].rearrange("p t (j c) -> p t j c", j=2),
                                rows[:, :, 0:S_CH].unsqueeze(2).to_broadcast([P, 2, 2, S_CH]),
                                ALU.mult).then_inc(prod_done, 1)

                        def accumulate(f, it, o, s):
                            base = dve.value_load(place_i[0:1, bass.ds(UNROLL * it + o, 1)], min_val=0, max_val=NPAD)
                            dve.wait_ge(turn_done, UNROLL * f + (o + 1))
                            if s != 0:
                                dve.wait_ge(acc_done, UNROLL * f + o)
                            at = bass.ds(base, WIN)
                            if own_weights:
                                t = turned[:, o % 2, :, :]
                                nc.vector.tensor_tensor(acc[:, 0:2, at], acc[:, 0:2, at], t[:, 0:2, 0:WIN], ALU.add)
                                nc.vector.tensor_tensor(acc[:, 2:8, at].rearrange("p (c k) n -> p c k n", c=2),
                                                        acc[:, 2:8, at].rearrange("p (c k) n -> p c k n", c=2),
                                                        t[:, 2:4, WIN:].rearrange("p c (k n) -> p c k n", k=3),
                                                        ALU.add).then_inc(acc_done, 1)
                            else:
                                t = turned[:, o % 2, 0:2, :].rearrange("p c (k n) -> p (c k) n", k=4)
                                nc.vector.tensor_tensor(acc[:, :, at], acc[:, :, at], t, ALU.add).then_inc(acc_done, 1)

                        def stage(f, it, o, s):
                            if s is None or s < GROUPS:
                                select(f, it, o, s)
                                if own_weights:
                                    products(f, o, 0)
                                    products(f, o, 1)
                            if s is None or s >= 2:
                                accumulate(f, it, o - 2, None if s is None else s - 2)

                        with passes(dve) as q:
                            stages(dve, q, stage, GROUPS + 2)
                            pass_over(dve, q)
                            nc.vector.tensor_scalar(rel[:], rel[:], float(WIN), None, ALU.subtract)
                            nc.vector.tensor_scalar(place[:], place[:], float(WIN), float(NPAD), ALU.add, ALU.min)
                            dve.drain()
                            nc.vector.tensor_copy(place_i[:], place[:])
                            dve.drain()

                    @block.tensor
                    def _(pe):
                        def hidden(f, o, s):
                            pe.wait_ge(feat_in[o % UNROLL], 16 * f + 16 * (o // UNROLL + 1))
                            if s is None or s >= 2:
                                pe.wait_ge(silu_done, UNROLL * f + (o - 1))
                            nc.tensor.matmul(hid_ps[:, o % 2, 0:GROUP // 2], fc1_sb[:], feat[:, o % UNROLL, :],
                                             start=True, stop=True).then_inc(hid_done, 1)

                        def edge_weights(f, o, h, s):
                            if h == 0:
                                pe.wait_ge(silu_done, UNROLL * f + (o + 1))
                            if s is None or s >= 1:
                                pe.wait_ge(prod_done, 2 * UNROLL * f + (2 * o + h - 1))
                            nc.tensor.matmul(w_ps[:, h, 0:2 * W_N], hid[:, o % 2, h * P:(h + 1) * P], fc2_sb[:],
                                             start=True, stop=True).then_inc(w_done, 1)

                        def aggregate(f, o, h, s):
                            if own_weights:
                                pe.wait_ge(prod_done, 2 * UNROLL * f + (2 * o + h + 1))
                            if h == 0:
                                pe.wait_ge(sel_done, UNROLL * f + (o + 1))
                                if s is None or s >= 2:
                                    pe.wait_ge(sums_copied, UNROLL * f + (o - 1))
                                if not own_weights:
                                    pe.wait_ge(gathered[o % UNROLL], 16 * TILES * f + 16 * TILES * (o // UNROLL + 1))
                            for j in (2 * h, 2 * h + 1):
                                rows = prod[:, o % 2, j, :] if own_weights else g[:, o % UNROLL, j, :]
                                last = nc.tensor.matmul(sums[:, o % 2, 0:width], sel[:, o % 2, j, :], rows,
                                                        start=(j == 0), stop=(j == TILES - 1))
                            last.then_inc(agg_done, 1)

                        def turn(f, o, s):
                            pe.wait_ge(sums_copied, UNROLL * f + (o + 1))
                            if s is None or s >= 2:
                                pe.wait_ge(acc_done, UNROLL * f + (o - 1))
                            v = sums_sb[:, o % 2, :]
                            if own_weights:
                                parts = [v[:, c:c + P] for c in LOW + HIGH]
                            else:
                                parts = [v[:, 0:P], v[:, D - P:D]]
                            for c, part in enumerate(parts):
                                last = nc.tensor.transpose(turned[:, o % 2, c, :], part, ident_sb[:])
                            last.then_inc(turn_done, 1)

                        def stage(f, it, o, s):
                            before = None if s is None else s - 1
                            if own_weights:
                                if s == 0:
                                    hidden(f, 0, 0)
                                if s is None or s < GROUPS:
                                    edge_weights(f, o, 0, s)
                                if s is None or 1 <= s <= GROUPS:
                                    aggregate(f, o - 1, 0, before)
                                if s is None or s + 1 < GROUPS:
                                    hidden(f, o + 1, None if s is None else s + 1)
                                if s is None or s < GROUPS:
                                    edge_weights(f, o, 1, s)
                                if s is None or s >= 2:
                                    turn(f, o - 2, None if s is None else s - 2)
                                if s is None or 1 <= s <= GROUPS:
                                    aggregate(f, o - 1, 1, before)
                            else:
                                if s is None or s < GROUPS:
                                    aggregate(f, o, 0, s)
                                    aggregate(f, o, 1, s)
                                if s is None or s >= 1:
                                    turn(f, o - 1, before)

                        with passes(pe) as q:
                            stages(pe, q, stage, GROUPS + 2 if own_weights else GROUPS + 1)
                            pass_over(pe, q)

        edge_passes(0)

        with ExitStack() as st:
            H = sb("h1", [P, NT, D], scope=st)
            pre = sb("pre", [P, 2, PRE], scope=st)
            sig = sb("sig", [P, 2, S_OUT], scope=st)
            val = sb("val", [P, 2, D], scope=st)
            node_ps = st.enter_context(nc.psum_tensor("node_ps0", [P, 2, 512], F32))
            node_done = sem("node0_done")
            pre_ready = sem("pre_ready")
            sig_ready = sem("sig_ready")
            val_ready = sem("val_ready")
            x_ready = sem("x_ready")
            h1_ready = sem("h1_ready")
            table_out = sem("table_out")
            cleared = sem("acc_cleared_again")
            win_step = sem("win_step")
            added = sem("added")

            norm_vector, norm_scalar = layer_norm("ln1", H, h1_ready, lambda e: e.wait_ge(x_ready, NT))
            with nc.Block() as block:
                @block.tensor
                def _(pe):
                    for t in range(NT):
                        if t >= 2:
                            pe.wait_ge(pre_ready, t - 1)
                        for m in range(PLANES):
                            last = nc.tensor.matmul(node_ps[:, t % 2, 0:PRE], acc[:, m, t * P:(t + 1) * P],
                                                    big0_sb[:, m, :], start=(m == 0), stop=(m == PLANES - 1))
                        last.then_inc(node_done, 1)

                @block.vector
                def _(dve):
                    for t in range(NT):
                        dve.wait_ge(node_done, t + 1)
                        if t >= 2:
                            dve.wait_ge(val_ready, t - 1)
                            dve.wait_ge(sig_ready, t - 1)
                        nc.vector.tensor_tensor(pre[:, t % 2, :], node_ps[:, t % 2, 0:PRE], sc[:, t, :],
                                                ALU.add).then_inc(pre_ready, 1)
                        dve.wait_ge(pre_ready, t + 1)
                        dve.wait_ge(sig_ready, t + 1)
                        if t >= 2:
                            dve.wait_ge(x_ready, t - 1)
                        nc.vector.scalar_tensor_tensor(out=val[:, t % 2, 0:S_CH], in0=pre[:, t % 2, 0:S_CH],
                                                       scalar=a_col[:, t:t + 1], in1=sig[:, t % 2, 0:S_CH],
                                                       op0=ALU.mult, op1=ALU.mult)
                        nc.vector.scalar_tensor_tensor(
                            out=val[:, t % 2, S_CH:D].rearrange("p (c i) -> p c i", i=3),
                            in0=pre[:, t % 2, S_OUT:PRE].rearrange("p (c i) -> p c i", i=3), scalar=a_col[:, t:t + 1],
                            in1=sig[:, t % 2, S_CH:S_OUT].unsqueeze(2).to_broadcast([P, V_CH, 3]),
                            op0=ALU.mult, op1=ALU.mult).then_inc(val_ready, 1)
                        dve.wait_ge(val_ready, t + 1)
                        nc.vector.tensor_tensor(X[:, t, :], X[:, t, :], val[:, t % 2, :], ALU.add).then_inc(x_ready, 1)
                    norm_vector(dve)
                    dve.wait_ge(h1_ready, 1)
                    nc.vector.tensor_tensor(X[:], X[:], H[:], ALU.add).then_inc(added, 1)
                    n = [0]

                    def then(ins):
                        n[0] += 1
                        ins.then_inc(win_step, 1)
                        dve.wait_ge(win_step, n[0])

                    windows(then)

                @block.scalar
                def _(act):
                    for t in range(NT):
                        act.wait_ge(pre_ready, t + 1)
                        if t >= 2:
                            act.wait_ge(val_ready, t - 1)
                        nc.scalar.activation(sig[:, t % 2, :], pre[:, t % 2, 0:S_OUT], ACT.Sigmoid,
                                             scale=a_col[:, t:t + 1]).then_inc(sig_ready, 1)
                    norm_scalar(act)

                @block.gpsimd
                def _(pool):
                    for t in range(NT):
                        pool.wait_ge(node_done, t + 1)
                        nc.gpsimd.memset(acc[:, :, t * P:(t + 1) * P], 0.0).then_inc(cleared, 1)
                    nc.gpsimd.memset(acc[:, :, NPAD:ACC_W], 0.0).then_inc(cleared, 1)
                    pool.wait_ge(cleared, NT + 1)

                @block.sync
                def _(sp):
                    sp.wait_ge(h1_ready, 1)
                    sp.dma_start(table_v[1], H[:]).then_inc(table_out, 16)
                    sp.wait_ge(table_out, 16)

        edge_passes(1)

        with ExitStack() as st:
            node_ps = st.enter_context(nc.psum_tensor("node_ps1", [P, 2, 512], F32))
            big1_sb = sb("big1_sb", [P, PLANES, D], scope=st)
            big1_in = sem("big1_in")
            node_done = sem("node1_done")
            y_ready = sem("y_ready")
            y_out = sem("y_out")
            with nc.Block() as block:
                @block.tensor
                def _(pe):
                    pe.wait_ge(big1_in, 16)
                    for t in range(NT):
                        if t >= 2:
                            pe.wait_ge(y_ready, t - 1)
                        for m in range(PLANES):
                            last = nc.tensor.matmul(node_ps[:, t % 2, 0:D], acc[:, m, t * P:(t + 1) * P],
                                                    big1_sb[:, m, :], start=(m == 0), stop=(m == PLANES - 1))
                        last.then_inc(node_done, 1)

                @block.vector
                def _(dve):
                    for t in range(NT):
                        dve.wait_ge(node_done, t + 1)
                        nc.vector.scalar_tensor_tensor(out=X[:, t, :], in0=node_ps[:, t % 2, 0:D], scalar=0.0,
                                                       in1=X[:, t, :], op0=ALU.max, op1=ALU.add).then_inc(y_ready, 1)

                @block.sync
                def _(sp):
                    sp.dma_start(big1_sb[:], big1_kept).then_inc(big1_in, 16)
                    for t in range(0, NT, 5):
                        sp.wait_ge(y_ready, t + 5)
                        sp.dma_start(out_v[:, t:t + 5, :], X[:, t:t + 5, :]).then_inc(y_out, 16)
                    sp.wait_ge(y_out, 16 * (NT // 5))


def _place_vec(to, w, rows, cols, ri, ci):
    n, m = w.shape
    to[rows + ri:rows + 3 * n:3, cols + ci:cols + 3 * m:3] = w


def _layer0_planes(ws, wv, sign):
    full = np.zeros((4, MSG, PRE), np.float32)
    full[0, C_W1:C_W1 + S_CH, 0:S_OUT] = ws[0:S_CH]
    for k in range(1, 4):
        full[k, C_W4 + k - 1:C_W4 + VC:3, 0:S_OUT] = ws[S_CH:]
    for i in range(3):
        a, b = (i + 1) % 3, (i + 2) % 3
        full[i + 1, C_W2:C_W2 + S_CH, S_OUT + i:PRE:3] = wv[0:64]
        full[0, C_W3 + i:C_W3 + VC:3, S_OUT + i:PRE:3] = wv[64:96]
        full[b + 1, C_W5 + a:C_W5 + VC:3, S_OUT + i:PRE:3] = wv[96:128]
        low = full[a + 1, C_W5 + b:C_W5 + VC:3, S_OUT + i:PRE:3]
        low[...] = wv[96:128]
        if sign:
            low *= -1
    planes = np.zeros((PLANES, P, PRE), np.float32)
    planes[0] = full[0, 0:P]
    planes[1, 0:C_W4 - P] = full[0, P:C_W4]
    for k in range(1, 4):
        planes[1 + k] = full[k, HIGH[0]:HIGH[0] + P]
        planes[4 + k] = full[k, HIGH[1]:HIGH[1] + P]
    return np.ascontiguousarray(planes.transpose(1, 0, 2))


def _layer1_pair(w1, w2, w3, w4, w5, sign):
    full = np.zeros((4, D, D), np.float32)
    full[0, 0:S_CH, 0:S_CH] = w1
    for i in range(3):
        a, b = (i + 1) % 3, (i + 2) % 3
        full[i + 1, S_CH + i:D:3, 0:S_CH] = w2
        full[i + 1, 0:S_CH, S_CH + i:D:3] = w3
        full[0, S_CH + i:D:3, S_CH + i:D:3] = w4
        full[b + 1, S_CH + a:D:3, S_CH + i:D:3] = w5
        low = full[a + 1, S_CH + b:D:3, S_CH + i:D:3]
        low[...] = w5
        if sign:
            low *= -1
    planes = np.zeros((2, 4, 2, P, P), np.float32)
    for k in range(4):
        t = np.zeros((2 * P, D), np.float32)
        t[0:D] = full[k].T
        for h in range(2):
            planes[0, k, h] = t[h * P:(h + 1) * P, 0:P]
            planes[1, k, h, :, 2 * P - D:] = t[h * P:(h + 1) * P, P:D]
    return np.ascontiguousarray(planes.reshape(2 * PLANES, P, P).transpose(1, 0, 2))


def _block_rows(full, overlap):
    n = full.shape[1]
    c = np.zeros((P, 2, n), np.float32)
    c[:, 0] = full[0:P]
    if overlap:
        c[2 * P - D:, 1] = full[P:D]
    else:
        c[0:D - P, 1] = full[P:D]
    return c


def _square(s, v):
    full = np.zeros((D, s.shape[1] + 3 * v.shape[1]), np.float32)
    full[0:S_CH, 0:s.shape[1]] = s
    for i in range(3):
        full[S_CH + i:D:3, s.shape[1] + i::3] = v
    return full


def _ones(value, *shape):
    return np.full(shape, value, np.float32)


def kernel(x, src, dst, edge_attr_4, edge_attr_64, node_vec1, L0_gnn_lin1_ws, L0_gnn_lin1_wv, L0_gnn_fc_w1,
           L0_gnn_fc_w2, L0_gnn_sc_ws, L0_gnn_sc_wv, L0_gnn_lin2_ws, L0_gnn_lin2_wv, L1_gnn_W1, L1_gnn_W2,
           L1_gnn_W3, L1_gnn_W4, L1_gnn_W5, L1_gnn_Ws, L1_gnn_Wv):
    import concourse.bacc as bacc
    from concourse.bass_utils import run_bass_kernel_spmd

    A = lambda v: np.asarray(v)

    def pad(v, n, mode="constant"):
        v = A(v)
        return np.pad(v, [(0, n - v.shape[0])] + [(0, 0)] * (v.ndim - 1), mode=mode)

    by_edge = lambda v: np.ascontiguousarray(np.moveaxis(v.reshape((GROUPS * TILES, P) + v.shape[1:]), 0, 1))
    order = lambda v: np.ascontiguousarray(v.reshape((GROUPS, 2, 2, P) + v.shape[1:]).swapaxes(1, 2).reshape(v.shape))
    e_src = order(pad(src, E_PAD))
    e_dst = order(pad(dst, E_PAD, "edge"))
    e_sh = order(pad(edge_attr_4, E_PAD))
    feat = pad(edge_attr_64, E_PAD).reshape(GROUPS, 2, GROUP // 2, S_CH).transpose(0, 1, 3, 2).reshape(GROUPS, P, GROUP // 2)

    f = float
    lin_sc = np.concatenate([_square(A(L0_gnn_lin1_ws), A(L0_gnn_lin1_wv)), _square(A(L0_gnn_sc_ws), A(L0_gnn_sc_wv))], 1)
    i_s, i_v = f(S_CH) ** -0.5, f(V_CH) ** -0.5
    lin_k = np.concatenate([_square(_ones(i_s, S_CH, S_CH), _ones(i_v, V_CH, V_CH)),
                            _square(_ones(i_s, S_CH, S_OUT), _ones(i_v, V_CH, V_CH))], 1)
    fc1 = np.zeros((P, P), np.float32)
    fc2 = np.zeros((P, 2 * W_N), np.float32)
    for h in range(2):
        fc1[h * 64:(h + 1) * 64, h * 64:(h + 1) * 64] = A(L0_gnn_fc_w1)
        fc2[h * 64:(h + 1) * 64, h * W_N:(h + 1) * W_N] = A(L0_gnn_fc_w2)
    k_s = 64.0 ** -0.5 * 16.0 ** -0.5 * 96.0 ** -0.5
    k_v = 64.0 ** -0.5 * 16.0 ** -0.5 * 128.0 ** -0.5
    ks = np.concatenate([_ones(k_s, 64, 96), _ones(k_s * 3.0 ** -0.5, 32, 96)])
    kv = np.concatenate([_ones(k_v, 96, 32), _ones(k_v * 2.0 ** -0.5, 32, 32)])
    c0, c1 = (S_CH + V_CH) ** -0.5, (3.0 / (S_CH + 2 * V_CH)) ** 0.5
    inv3, inv6 = 3.0 ** -0.5, 6.0 ** -0.5

    arrays = {
        "x": pad(x, NPAD),
        "node_vec": np.ascontiguousarray(pad(node_vec1, NPAD).reshape(NT, P).T),
        "src_idx": np.ascontiguousarray(e_src.reshape(GROUPS // 2, 2 * TILES, P).transpose(0, 2, 1)),
        "dst_idx": by_edge(e_dst),
        "edge_sh": by_edge(e_sh),
        "edge_feat": np.ascontiguousarray(feat),
        "ident": np.eye(P, dtype=np.float32),
        "iota": np.tile(np.arange(WIN, dtype=np.float32), (P, 1)),
        "lin_sc": _block_rows(lin_sc, True),
        "lin_sc_scale": _block_rows(lin_k, True),
        "fc1": fc1,
        "fc2": fc2,
        "big0": _layer0_planes(A(L0_gnn_lin2_ws), A(L0_gnn_lin2_wv), False),
        "big0_scale": _layer0_planes(ks, kv, True),
        "l1_pair": _layer1_pair(A(L1_gnn_W1), A(L1_gnn_W2), A(L1_gnn_W3), A(L1_gnn_W4), A(L1_gnn_W5), False),
        "l1_pair_scale": _layer1_pair(_ones(c0, 64, 64), _ones(c0 * inv3, 32, 64), _ones(c1 * inv3, 64, 32),
                                      _ones(c1 * inv3, 32, 32), _ones(c1 * inv6, 32, 32), True),
        "l1_out": _block_rows(_square(A(L1_gnn_Ws), A(L1_gnn_Wv)), False),
        "l1_out_scale": _block_rows(_square(_ones(i_s, 64, 64), _ones(i_v, 32, 32)), False),
    }
    nc = bacc.Bacc("TRN2", target_bir_lowering=False, num_devices=1)
    args = [nc.dram_tensor(n + "_dram", v.shape, mybir.dt.from_np(v.dtype), kind="ExternalInput").ap()
            for n, v in arrays.items()]
    out = nc.dram_tensor("out_dram", (NPAD, D), F32, kind="ExternalOutput").ap()
    build(nc, *args, out)
    r = run_bass_kernel_spmd(nc, [{n + "_dram": v for n, v in arrays.items()}], core_ids=[0])
    return r.results[0]["out_dram"][0:N]
```

```python
import numpy as np
from contextlib import ExitStack

import concourse.bass as bass
from concourse import mybir

F32 = mybir.dt.float32
I32 = mybir.dt.int32
ALU = mybir.AluOpType
ACT = mybir.ActivationFunctionType
AXX = mybir.AxisListType.X
RMAX = bass.bass_isa.ReduceOp.max

P = 128
N = 3125
E = 103125
NT = -(-N // P)
NPAD = NT * P
S_CH, V_CH = 64, 32
VC = 3 * V_CH
D = S_CH + VC
W_N = 2 * S_CH + 3 * V_CH
S_OUT = 96
PRE = S_OUT + VC
MSG = 2 * S_CH + 3 * VC
TILES = 4
GROUP = TILES * P
UNROLL = 4
GROUPS = -(-E // (GROUP * UNROLL)) * UNROLL
ITERS = GROUPS // UNROLL
E_PAD = GROUPS * GROUP
WIN = 32
ACC_W = NPAD + WIN
PLANES = 8
EPS = 1e-5

C_W1, C_W3, C_W4, C_W5, C_W2 = 0, S_CH, S_CH + VC, S_CH + 2 * VC, S_CH + 3 * VC
HIGH_N = MSG - C_W4
BATCH = 5


def build(nc, x, node_vec, src_idx, dst_idx, edge_sh, edge_feat, ident, iota, lin_sc, lin_sc_scale,
          fc1, fc2, big0, big0_scale, l1_pair, l1_pair_scale, l1_out, l1_out_scale, out):
    table = [nc.dram_tensor(f"node_table_{l}", (NPAD, D), F32, kind="Internal").ap() for l in range(2)]
    big1_kept = nc.dram_tensor("big1_kept", (P, PLANES, D), F32, kind="Internal").ap()
    x_v = x.rearrange("(n p) c -> p n c", p=P)
    out_v = out.rearrange("(n p) c -> p n c", p=P)
    table_v = [t.rearrange("(n p) c -> p n c", p=P) for t in table]

    ctx = ExitStack()
    with ctx:
        def sb(name, shape, dt=F32, scope=ctx):
            return scope.enter_context(nc.sbuf_tensor(name, shape, dt))

        def sem(name):
            return ctx.enter_context(nc.semaphore(name))

        acc = sb("acc", [P, PLANES, ACC_W])
        X = sb("X", [P, NT, D])
        sc = sb("sc", [P, NT, PRE])
        a_col = sb("a_col", [P, NT])
        dst = sb("dst", [P, GROUPS * TILES], I32)
        rel = sb("rel", [P, GROUPS * TILES])
        sh = sb("sh", [P, GROUPS * TILES, 4])
        first = sb("first", [P, GROUPS])
        place = sb("place", [1, GROUPS])
        place_i = sb("place_i", [1, GROUPS], I32)
        turns_f = sb("turns_f", [1, 1])
        turns_i = sb("turns_i", [1, 3], I32)
        ident_sb = sb("ident_sb", [P, P])
        iota_sb = sb("iota_sb", [P, WIN])
        fc1_sb = sb("fc1_sb", [P, P])
        fc2_sb = sb("fc2_sb", [P, 2 * W_N])
        big0_sb = sb("big0_sb", [P, PLANES, PRE])
        stats = sb("stats", [P, NT, 6])
        mean_var = sb("mean_var", [P, NT, 2])
        rstd = sb("rstd", [P, NT])
        eps_col = sb("eps_col", [P, 1])

        def spread(dve, tiles, n, done, ready):
            for t in tiles:
                last = nc.vector.bn_stats(stats[:, t, :], X[:, t, :])
            last.then_inc(done, 1)
            dve.wait_ge(done, n + 1)
            for t in tiles:
                last = nc.vector.bn_aggr(mean_var[:, t, :], stats[:, t, :])
            last.then_inc(ready, 1)

        def root(tiles, ready):
            nc.scalar.activation(rstd[:, tiles[0]:tiles[-1] + 1], mean_var[:, tiles[0]:tiles[-1] + 1, 1], ACT.Sqrt,
                                 bias=eps_col[:, 0:1]).then_inc(ready, 1)

        def normalise(H, t):
            return nc.vector.tensor_scalar(H[:, t, :], X[:, t, :], mean_var[:, t, 0:1], rstd[:, t:t + 1],
                                           ALU.subtract, ALU.mult)

        def windows(then):
            wide = [P, GROUPS, TILES]
            then(nc.vector.tensor_tensor(rel[:].rearrange("p (g t) -> p g t", t=TILES),
                                         dst[:].rearrange("p (g t) -> p g t", t=TILES),
                                         first[:].unsqueeze(2).to_broadcast(wide), ALU.subtract))
            then(nc.vector.tensor_copy(place[:], first[0:1, :]))
            then(nc.vector.tensor_copy(place_i[:], place[:]))

        with ExitStack() as st:
            H = sb("h0", [P, NT, D], scope=st)
            hT = sb("hT", [P, 2, 2, P], scope=st)
            rows = sb("rows", [P, 2, D], scope=st)
            big1 = sb("big1", [P, PLANES, D], scope=st)
            lin = sb("lin", [P, 2, D + PRE], scope=st)
            lin_k = sb("lin_k", [P, 2, D + PRE], scope=st)
            wout = sb("wout", [P, 2, D], scope=st)
            wout_k = sb("wout_k", [P, 2, D], scope=st)
            least = sb("least", [P, 2, GROUPS], scope=st)
            both = sb("both", [P, 2, GROUPS], scope=st)
            spare = acc[:, PLANES - 2:PLANES, :].rearrange("p a n -> p (a n)")
            n_pair, n_big = 2 * PLANES * P, PLANES * PRE
            pair = spare[:, 0:n_pair].rearrange("p (m n) -> p m n", n=P)
            pair_k = spare[:, n_pair:2 * n_pair].rearrange("p (m n) -> p m n", n=P)
            big_k = spare[:, 2 * n_pair:2 * n_pair + n_big].rearrange("p (c n) -> p c n", c=PLANES)
            span = spare[:, 2 * n_pair + n_big:2 * n_pair + n_big + GROUPS]
            tp = st.enter_context(nc.psum_tensor("tp", [P, 2, 2, 256], F32))
            mm = st.enter_context(nc.psum_tensor("mm", [P, 4, 512], F32))
            cp = st.enter_context(nc.psum_tensor("cp", [P, 2, 512], F32))
            BANKS, LAG, MID = 4, 3, 4

            x_in = [sem(f"x_in{b}") for b in range(NT // BATCH)]
            dst_in = sem("dst_in")
            lin_in = sem("lin_in")
            w_in = sem("w_in")
            edges_in = sem("edges_in")
            eps_set = sem("eps_set")
            stats_step = sem("stats_step")
            var_ready = sem("var_ready")
            root_ready = sem("root_ready")
            rstd_ready = sem("rstd_ready")
            h0_ready = sem("h0_ready")
            lin_ready = sem("lin_ready")
            least_ready = sem("least_ready")
            both_ready = sem("both_ready")
            weights_ready = sem("weights_ready")
            hT_turned = sem("hT_turned")
            hT_ready = sem("hT_ready")
            lin_done = sem("lin_done")
            rows_ready = sem("rows_ready")
            sc_ready = sem("sc_ready")
            rows_out = [sem(f"rows_out{i}") for i in range(2)]
            comp_done = sem("comp_done")
            comp_copied = sem("comp_copied")
            big1_out = sem("big1_out")
            windows_set = sem("windows_set")
            acc_clear = sem("acc_clear")
            setup_step = sem("setup_step")
            batches = [range(b, b + BATCH) for b in range(0, NT, BATCH)]

            with nc.Block() as block:
                @block.sync
                def _(sp):
                    for b, tiles in enumerate(batches):
                        sp.dma_start(X[:, tiles[0]:tiles[-1] + 1, :], x_v[:, tiles[0]:tiles[-1] + 1, :]).then_inc(x_in[b], 16)
                    sp.dma_start(a_col[:], node_vec).then_inc(lin_in, 16)
                    sp.dma_start(dst[:], dst_idx).then_inc(dst_in, 16)
                    sp.dma_start(pair, l1_pair).then_inc(w_in, 16)
                    sp.dma_start(pair_k, l1_pair_scale).then_inc(w_in, 16)
                    sp.dma_start(wout[:], l1_out).then_inc(w_in, 16)
                    sp.dma_start(wout_k[:], l1_out_scale).then_inc(w_in, 16)
                    sp.dma_start(big0_sb[:], big0).then_inc(w_in, 16)
                    sp.dma_start(big_k, big0_scale).then_inc(w_in, 16)
                    sp.dma_start(iota_sb[:], iota).then_inc(edges_in, 16)
                    sp.dma_start(fc1_sb[:], fc1).then_inc(edges_in, 16)
                    sp.dma_start(fc2_sb[:], fc2).then_inc(edges_in, 16)
                    sp.dma_start(sh[:], edge_sh).then_inc(edges_in, 16)
                    for t in range(NT):
                        sp.wait_ge(rows_ready, t + 1)
                        sp.dma_start(table_v[0][:, t, :], rows[:, t % 2, :]).then_inc(rows_out[t % 2], 16)
                    sp.wait_ge(comp_copied, PLANES // 2)
                    sp.dma_start(big1_kept, big1[:]).then_inc(big1_out, 16)
                    sp.wait_ge(big1_out, 16)
                    sp.wait_ge(rows_out[0], 16 * ((NT + 1) // 2))
                    sp.wait_ge(rows_out[1], 16 * (NT // 2))
                    sp.wait_ge(edges_in, 64)

                @block.gpsimd
                def _(pool):
                    nc.gpsimd.memset(acc[:, 0:PLANES - 2, :], 0.0).then_inc(acc_clear, 1)
                    pool.wait_ge(least_ready, 1)
                    nc.gpsimd.partition_all_reduce(both[:].rearrange("p a g -> p (a g)"),
                                                   least[:].rearrange("p a g -> p (a g)"), P, RMAX).then_inc(both_ready, 1)
                    pool.wait_ge(comp_done, PLANES // 2)
                    pool.wait_ge(windows_set, 1)
                    nc.gpsimd.memset(acc[:, PLANES - 2:PLANES, :], 0.0).then_inc(acc_clear, 1)
                    pool.wait_ge(acc_clear, 2)

                @block.vector
                def _(dve):
                    n = [0]

                    def then(ins):
                        n[0] += 1
                        ins.then_inc(setup_step, 1)
                        dve.wait_ge(setup_step, n[0])

                    nc.vector.memset(eps_col[:], EPS).then_inc(eps_set, 1)
                    for b, tiles in enumerate(batches):
                        dve.wait_ge(x_in[b], 16)
                        spread(dve, tiles, b, stats_step, var_ready)
                    dve.wait_ge(lin_in, 64)
                    nc.vector.tensor_tensor(lin[:], lin[:], lin_k[:], ALU.mult).then_inc(lin_ready, 1)
                    dve.wait_ge(root_ready, len(batches))
                    nc.vector.reciprocal(rstd[:], rstd[:]).then_inc(rstd_ready, 1)
                    dve.wait_ge(rstd_ready, 1)
                    for t in range(NT + LAG):
                        if t < NT:
                            normalise(H, t).then_inc(h0_ready, 1)
                        if t >= LAG:
                            u = t - LAG
                            dve.wait_ge(lin_done, u + 1)
                            if u >= 2:
                                dve.wait_ge(rows_out[u % 2], 16 * (u // 2))
                            nc.vector.tensor_scalar(rows[:, u % 2, :], mm[:, u % BANKS, 0:D], a_col[:, u:u + 1],
                                                    None, ALU.mult).then_inc(rows_ready, 1)
                            nc.vector.tensor_copy(sc[:, u, :], mm[:, u % BANKS, D:D + PRE]).then_inc(sc_ready, 1)
                        if t == MID:
                            dve.wait_ge(w_in, 6 * 16)
                            nc.vector.tensor_tensor(pair, pair, pair_k, ALU.mult)
                            nc.vector.tensor_tensor(wout[:], wout[:], wout_k[:], ALU.mult).then_inc(weights_ready, 1)
                        if t == MID + 1:
                            then(nc.vector.tensor_tensor(big0_sb[:], big0_sb[:], big_k, ALU.mult))
                            dve.wait_ge(dst_in, 16)
                            by_group = dst[:].rearrange("p (g t) -> p g t", t=TILES)
                            then(nc.vector.tensor_reduce(least[:, 0, :], by_group, AXX, ALU.min))
                            then(nc.vector.tensor_scalar(least[:, 0, :], least[:, 0, :], -1.0, None, ALU.mult))
                            nc.vector.tensor_reduce(least[:, 1, :], by_group, AXX, ALU.max).then_inc(least_ready, 1)
                        if t == MID + 7:
                            dve.wait_ge(both_ready, 1)
                            then(nc.vector.tensor_scalar(first[:], both[:, 0, :], -1.0, None, ALU.mult))
                            then(nc.vector.tensor_tensor(span, both[:, 0, :], both[:, 1, :], ALU.add))
                            then(nc.vector.tensor_reduce(turns_f[:], span[0:1, :], AXX, ALU.max))
                            then(nc.vector.tensor_copy(turns_i[:, 0:1], turns_f[:]))
                            then(nc.vector.tensor_scalar(turns_i[:, 1:2], turns_i[:, 0:1], WIN.bit_length() - 1, None,
                                                         ALU.arith_shift_right))
                            then(nc.vector.tensor_scalar(turns_i[:, 2:3], turns_i[:, 1:2], float(ITERS), float(ITERS),
                                                         ALU.mult, ALU.add))
                            windows(then)
                            nc.vector.tensor_copy(place_i[:], place[:]).then_inc(windows_set, 1)

                @block.scalar
                def _(act):
                    act.dma_start(lin[:], lin_sc).then_inc(lin_in, 16)
                    act.dma_start(lin_k[:], lin_sc_scale).then_inc(lin_in, 16)
                    act.dma_start(ident_sb[:], ident).then_inc(lin_in, 16)
                    act.wait_ge(eps_set, 1)
                    for b, tiles in enumerate(batches):
                        act.wait_ge(var_ready, b + 1)
                        root(tiles, root_ready)
                    for t in range(NT):
                        act.wait_ge(hT_turned, t + 1)
                        if t >= 2:
                            act.wait_ge(lin_done, t - 1)
                        nc.scalar.activation(hT[:, t % 2, :, :], tp[:, t % 2, :, 0:P], ACT.Relu).then_inc(hT_ready, 1)
                        if t == MID:
                            for m in range(PLANES // 2):
                                act.wait_ge(comp_done, m + 1)
                                nc.scalar.activation(big1[:, 2 * m:2 * m + 2, :],
                                                     cp[:, m % 2, 0:2 * D].rearrange("p (c n) -> p c n", c=2),
                                                     ACT.Copy).then_inc(comp_copied, 1)

                @block.tensor
                def _(pe):
                    pe.wait_ge(lin_ready, 1)
                    for t in range(NT + 1):
                        if t < NT:
                            pe.wait_ge(h0_ready, t + 1)
                            if t >= 2:
                                pe.wait_ge(hT_ready, t - 1)
                            nc.tensor.transpose(tp[:, t % 2, 0, 0:P], H[:, t, 0:P], ident_sb[:])
                            nc.tensor.transpose(tp[:, t % 2, 1, 0:P], H[:, t, D - P:D], ident_sb[:]).then_inc(hT_turned, 1)
                        if t >= 1:
                            u = t - 1
                            pe.wait_ge(hT_ready, u + 1)
                            if u >= BANKS:
                                pe.wait_ge(rows_ready, u - BANKS + 1)
                                pe.wait_ge(sc_ready, u - BANKS + 1)
                            for c in range(2):
                                last = nc.tensor.matmul(mm[:, u % BANKS, 0:D + PRE], hT[:, u % 2, c, :], lin[:, c, :],
                                                        start=(c == 0), stop=(c == 1))
                            last.then_inc(lin_done, 1)
                        if t == MID:
                            pe.wait_ge(weights_ready, 1)
                            for m in range(PLANES // 2):
                                if m >= 2:
                                    pe.wait_ge(comp_copied, m - 1)
                                for h in range(2):
                                    for c in range(2):
                                        last = nc.tensor.matmul(cp[:, m % 2, h * D:(h + 1) * D],
                                                                pair[:, 2 * (2 * m + h) + c, :], wout[:, c, :],
                                                                start=(c == 0), stop=(c == 1))
                                last.then_inc(comp_done, 1)

        def edge_passes(layer):
            L = f"l{layer}_"
            own_weights = layer == 0
            width = HIGH_N if own_weights else D
            with ExitStack() as st:
                idx = sb(L + "idx", [P, 2, 2 * TILES], I32, scope=st)
                g = sb(L + "g", [P, UNROLL, TILES, D], scope=st)
                hot = sb(L + "hot", [P, 2, TILES, WIN], scope=st)
                sel = sb(L + "sel", [P, 2, TILES, 4 * WIN], scope=st)
                sums_sb = sb(L + "sums_sb", [P, 2, width], scope=st)
                sums = st.enter_context(nc.psum_tensor(L + "sums", [P, 2, 512], F32))
                turned = st.enter_context(nc.psum_tensor(L + "turned", [P, 2, 4, P], F32))
                if own_weights:
                    feat = sb(L + "feat", [P, UNROLL, GROUP // 2], scope=st)
                    hid = sb(L + "hid", [P, 2, GROUP // 2], scope=st)
                    prod = sb(L + "prod", [P, 2, TILES, MSG], scope=st)
                    hid_ps = st.enter_context(nc.psum_tensor(L + "hid_ps", [P, 2, 512], F32))
                    w_ps = st.enter_context(nc.psum_tensor(L + "w_ps", [P, 2, 512], F32))

                idx_in = [sem(L + f"idx_in{h}") for h in range(2)]
                feat_in = [sem(L + f"feat_in{u}") for u in range(UNROLL)]
                gathered = [sem(L + f"gathered{u}") for u in range(UNROLL)]
                hid_done = sem(L + "hid_done")
                silu_done = sem(L + "silu_done")
                w_done = sem(L + "w_done")
                prod_done = sem(L + "prod_done")
                hot_done = sem(L + "hot_done")
                sel_done = sem(L + "sel_done")
                agg_done = sem(L + "agg_done")
                sums_copied = sem(L + "sums_copied")
                turn_done = sem(L + "turn_done")
                acc_done = sem(L + "acc_done")
                gather_begun = sem(L + "gather_begun")
                pass_left = sem(L + "pass_left")

                def passes(eng):
                    total = eng.value_load(turns_i[0:1, 2:3], min_val=ITERS, max_val=ITERS * (-(-N // WIN)))
                    return eng.Fori(0, total, ITERS)

                def pass_over(eng, q):
                    end = eng.snap(UNROLL * q + GROUPS)
                    eng.wait_ge(acc_done, end)
                    eng.sem_inc(pass_left, 1)

                def stages(eng, q, stage, last):
                    for s in range(UNROLL):
                        stage(q, 0, s, s)
                    with eng.Fori(1, ITERS - 1) as it:
                        f = eng.snap(q + it)
                        for o in range(UNROLL):
                            stage(f, it, o, None)
                    f = eng.snap(q + (ITERS - 1))
                    for s in range(GROUPS - UNROLL, last):
                        stage(f, ITERS - 1, s - (GROUPS - UNROLL), s)

                with nc.Block() as block:
                    @block.sync
                    def _(sp):
                        def load_idx(pair, h):
                            sp.dma_start(idx[:, h, :], src_idx[bass.ds(pair, 1), :, :].rearrange("a p t -> (a p) t")).then_inc(idx_in[h], 16)

                        def load_feat(group, u):
                            sp.dma_start(feat[:, u, :], edge_feat[bass.ds(group, 1), :, :].rearrange("a p c -> (a p) c")).then_inc(feat_in[u], 16)

                        with passes(sp) as q:
                            for h in range(2):
                                load_idx(h, h)
                            if own_weights:
                                for u in range(UNROLL):
                                    load_feat(u, u)
                            with sp.Fori(0, ITERS - 1) as it:
                                f = sp.snap(q + it)
                                for u in range(UNROLL):
                                    group = sp.snap(UNROLL * it + (UNROLL + u))
                                    if u % 2:
                                        pair = sp.snap(2 * it + (2 + u // 2))
                                        rows = sp.snap(16 * TILES * f + 16 * TILES)
                                        sp.wait_ge(gathered[u - 1], rows)
                                        sp.wait_ge(gathered[u], rows)
                                        load_idx(pair, u // 2)
                                    if own_weights:
                                        used = sp.snap(UNROLL * f + (u + 1))
                                        sp.wait_ge(hid_done, used)
                                        load_feat(group, u)
                            pass_over(sp, q)

                    @block.gpsimd
                    def _(pool):
                        def gather(f, u, full):
                            used = pool.snap(2 * UNROLL * f + (2 * u + 2 - 2 * UNROLL)) if full else None
                            there = pool.snap(16 * f + 16)
                            if u % 2 == 0:
                                pool.wait_ge(idx_in[u // 2], there)
                            if full:
                                pool.wait_ge(prod_done if own_weights else agg_done, used)
                            if full or u % 2 == 0:
                                pool.sem_inc(gather_begun, 1)
                            for j in range(TILES):
                                nc.gpsimd.indirect_dma_start(
                                    out=g[:, u, j, :], out_offset=None, in_=table[layer],
                                    in_offset=bass.IndirectOffsetOnAxis(ap=idx[:, u // 2, (u % 2) * TILES + j:(u % 2) * TILES + j + 1], axis=0),
                                ).then_inc(gathered[u], 16)

                        with passes(pool) as q:
                            for u in range(UNROLL):
                                gather(q, u, False)
                            with pool.Fori(1, ITERS) as it:
                                f = pool.snap(q + it)
                                for u in range(UNROLL):
                                    gather(f, u, True)
                            pass_over(pool, q)

                    @block.scalar
                    def _(act):
                        def silu(f, o, s):
                            act.wait_ge(hid_done, UNROLL * f + (o + 1))
                            if s is None or s >= 2:
                                act.wait_ge(w_done, 2 * UNROLL * f + (2 * o - 2))
                            nc.scalar.activation(hid[:, o % 2, :], hid_ps[:, o % 2, 0:GROUP // 2], ACT.Silu,
                                                 scale=float(S_CH) ** -0.5).then_inc(silu_done, 1)

                        def copy_sums(f, o, s):
                            act.wait_ge(agg_done, 2 * UNROLL * f + (2 * o + 2))
                            if s is None or s >= 2:
                                act.wait_ge(turn_done, UNROLL * f + (o - 1))
                            nc.scalar.activation(sums_sb[:, o % 2, :], sums[:, o % 2, 0:width], ACT.Copy).then_inc(sums_copied, 1)

                        def stage(f, it, o, s):
                            if own_weights:
                                if s == 0:
                                    silu(f, 0, 0)
                                if s is None or s >= 2:
                                    copy_sums(f, o - 2, None if s is None else s - 2)
                                if s is None or s + 1 < GROUPS:
                                    silu(f, o + 1, None if s is None else s + 1)
                            else:
                                copy_sums(f, o, s)

                        with passes(act) as q:
                            stages(act, q, stage, GROUPS + 2 if own_weights else GROUPS)
                            pass_over(act, q)

                    @block.vector
                    def _(dve):
                        def select(f, it, o, s):
                            if s is None or s >= 2:
                                dve.wait_ge(agg_done, 2 * UNROLL * f + (2 * o - 2))
                            at = bass.ds(UNROLL * TILES * it + TILES * o, TILES)
                            nc.vector.tensor_tensor(hot[:, o % 2, :, :], iota_sb[:].unsqueeze(1).to_broadcast([P, TILES, WIN]),
                                                    rel[:, at].unsqueeze(2).to_broadcast([P, TILES, WIN]),
                                                    ALU.is_equal).then_inc(hot_done, 1)
                            dve.wait_ge(hot_done, UNROLL * f + (o + 1))
                            nc.vector.tensor_tensor(sel[:, o % 2, :, :].rearrange("p t (k n) -> p t k n", k=4),
                                                    hot[:, o % 2, :, :].unsqueeze(2).to_broadcast([P, TILES, 4, WIN]),
                                                    sh[:, at, :].unsqueeze(3).to_broadcast([P, TILES, 4, WIN]),
                                                    ALU.mult).then_inc(sel_done, 1)

                        def products(f, o, h):
                            u = o % UNROLL
                            dve.wait_ge(w_done, 2 * UNROLL * f + (2 * o + h + 1))
                            if h == 0:
                                dve.wait_ge(gathered[u], 16 * TILES * f + 16 * TILES * (o // UNROLL + 1))
                            w = w_ps[:, h, 0:2 * W_N].rearrange("p (t c) -> p t c", t=2)
                            rows = g[:, u, 2 * h:2 * h + 2, :]
                            to = prod[:, o % 2, 2 * h:2 * h + 2, :]
                            s_cols = to[:, :, 0:S_CH]
                            both = bass.AP(s_cols.tensor, s_cols.offset,
                                           [*s_cols.ap[0:2], [C_W2 - C_W1, 2], s_cols.ap[2]])
                            for t in range(2):
                                nc.vector.tensor_tensor(
                                    to[:, t, C_W3:C_W2].rearrange("p (j c i) -> p j c i", j=3, i=3),
                                    w[:, t, 2 * S_CH:W_N].rearrange("p (j c) -> p j c", j=3).unsqueeze(3).to_broadcast([P, 3, V_CH, 3]),
                                    rows[:, t, S_CH:D].rearrange("p (c i) -> p c i", i=3).unsqueeze(1).to_broadcast([P, 3, V_CH, 3]),
                                    ALU.mult)
                            nc.vector.tensor_tensor(
                                both,
                                w[:, :, 0:2 * S_CH].rearrange("p t (j c) -> p t j c", j=2),
                                rows[:, :, 0:S_CH].unsqueeze(2).to_broadcast([P, 2, 2, S_CH]),
                                ALU.mult).then_inc(prod_done, 1)

                        def accumulate(f, it, o, s):
                            base = dve.value_load(place_i[0:1, bass.ds(UNROLL * it + o, 1)], min_val=0, max_val=NPAD)
                            dve.wait_ge(turn_done, UNROLL * f + (o + 1))
                            if s != 0:
                                dve.wait_ge(acc_done, UNROLL * f + o)
                            at = bass.ds(base, WIN)
                            t = turned[:, o % 2, 0:2, :].rearrange("p c (k n) -> p (c k) n", k=4)
                            nc.vector.tensor_tensor(acc[:, :, at], acc[:, :, at], t, ALU.add).then_inc(acc_done, 1)

                        def stage(f, it, o, s):
                            if s is None or s < GROUPS:
                                select(f, it, o, s)
                                if own_weights:
                                    products(f, o, 0)
                                    products(f, o, 1)
                            if s is None or s >= 2:
                                accumulate(f, it, o - 2, None if s is None else s - 2)

                        with passes(dve) as q:
                            stages(dve, q, stage, GROUPS + 2)
                            pass_over(dve, q)
                            nc.vector.tensor_scalar(rel[:], rel[:], float(WIN), None, ALU.subtract)
                            nc.vector.tensor_scalar(place[:], place[:], float(WIN), float(NPAD), ALU.add, ALU.min)
                            dve.drain()
                            nc.vector.tensor_copy(place_i[:], place[:])
                            dve.drain()

                    @block.tensor
                    def _(pe):
                        def hidden(f, o, s):
                            pe.wait_ge(feat_in[o % UNROLL], 16 * f + 16 * (o // UNROLL + 1))
                            if s is None or s >= 2:
                                pe.wait_ge(silu_done, UNROLL * f + (o - 1))
                            nc.tensor.matmul(hid_ps[:, o % 2, 0:GROUP // 2], fc1_sb[:], feat[:, o % UNROLL, :],
                                             start=True, stop=True).then_inc(hid_done, 1)

                        def edge_weights(f, o, h, s):
                            if h == 0:
                                pe.wait_ge(silu_done, UNROLL * f + (o + 1))
                            if s is None or s >= 1:
                                pe.wait_ge(prod_done, 2 * UNROLL * f + (2 * o + h - 1))
                            nc.tensor.matmul(w_ps[:, h, 0:2 * W_N], hid[:, o % 2, h * P:(h + 1) * P], fc2_sb[:],
                                             start=True, stop=True).then_inc(w_done, 1)

                        def aggregate(f, o, h, s):
                            if own_weights:
                                pe.wait_ge(prod_done, 2 * UNROLL * f + (2 * o + h + 1))
                            if h == 0:
                                pe.wait_ge(sel_done, UNROLL * f + (o + 1))
                                if s is None or s >= 2:
                                    pe.wait_ge(sums_copied, UNROLL * f + (o - 1))
                                if not own_weights:
                                    pe.wait_ge(gathered[o % UNROLL], 16 * TILES * f + 16 * TILES * (o // UNROLL + 1))
                            for j in (2 * h, 2 * h + 1):
                                first_last = dict(start=(j == 0), stop=(j == TILES - 1))
                                if own_weights:
                                    for k in range(4):
                                        c = C_W4 if k else C_W1
                                        at = slice(k * WIN, (k + 1) * WIN)
                                        last = nc.tensor.matmul(sums[at, o % 2, 0:HIGH_N], sel[:, o % 2, j, at],
                                                                prod[:, o % 2, j, c:c + HIGH_N],
                                                                tile_position=(0, k * WIN), **first_last)
                                else:
                                    last = nc.tensor.matmul(sums[:, o % 2, 0:D], sel[:, o % 2, j, :],
                                                            g[:, o % UNROLL, j, :], **first_last)
                            last.then_inc(agg_done, 1)

                        def turn(f, o, s):
                            pe.wait_ge(sums_copied, UNROLL * f + (o + 1))
                            if s is None or s >= 2:
                                pe.wait_ge(acc_done, UNROLL * f + (o - 1))
                            v = sums_sb[:, o % 2, :]
                            parts = [v[:, 0:P], v[:, width - P:width]]
                            for c, part in enumerate(parts):
                                last = nc.tensor.transpose(turned[:, o % 2, c, :], part, ident_sb[:])
                            last.then_inc(turn_done, 1)

                        def stage(f, it, o, s):
                            before = None if s is None else s - 1
                            if own_weights:
                                if s == 0:
                                    hidden(f, 0, 0)
                                if s is None or s < GROUPS:
                                    edge_weights(f, o, 0, s)
                                if s is None or 1 <= s <= GROUPS:
                                    aggregate(f, o - 1, 0, before)
                                if s is None or s + 1 < GROUPS:
                                    hidden(f, o + 1, None if s is None else s + 1)
                                if s is None or s < GROUPS:
                                    edge_weights(f, o, 1, s)
                                if s is None or s >= 2:
                                    turn(f, o - 2, None if s is None else s - 2)
                                if s is None or 1 <= s <= GROUPS:
                                    aggregate(f, o - 1, 1, before)
                            else:
                                if s is None or s < GROUPS:
                                    aggregate(f, o, 0, s)
                                    aggregate(f, o, 1, s)
                                if s is None or s >= 1:
                                    turn(f, o - 1, before)

                        with passes(pe) as q:
                            stages(pe, q, stage, GROUPS + 2 if own_weights else GROUPS + 1)
                            pass_over(pe, q)

        edge_passes(0)

        with ExitStack() as st:
            H = sb("h1", [P, NT, D], scope=st)
            pre = sb("pre", [P, 2, PRE], scope=st)
            sig = sb("sig", [P, 2, S_OUT], scope=st)
            val = sb("val", [P, 2, D], scope=st)
            node_ps = st.enter_context(nc.psum_tensor("node_ps0", [P, 4, 512], F32))
            node_done = sem("node0_done")
            pre_ready = sem("pre_ready")
            sig_ready = sem("sig_ready")
            val_ready = sem("val_ready")
            x_ready = sem("x_ready")
            stats_step1 = sem("stats_step1")
            var_ready1 = sem("var_ready1")
            root_ready1 = sem("root_ready1")
            rstd_ready1 = sem("rstd_ready1")
            norm_ready = sem("norm_ready")
            h1_ready = sem("h1_ready")
            table_out = sem("table_out")
            cleared = sem("acc_cleared_again")
            win_step = sem("win_step")
            added = sem("added")
            BANKS = 4
            batches = [range(b, b + BATCH) for b in range(0, NT, BATCH)]

            with nc.Block() as block:
                @block.tensor
                def _(pe):
                    for t in range(NT):
                        if t >= BANKS:
                            pe.wait_ge(pre_ready, t - BANKS + 1)
                        for m in range(PLANES):
                            last = nc.tensor.matmul(node_ps[:, t % BANKS, 0:PRE], acc[:, m, t * P:(t + 1) * P],
                                                    big0_sb[:, m, :], start=(m == 0), stop=(m == PLANES - 1))
                        last.then_inc(node_done, 1)

                @block.vector
                def _(dve):
                    n = [0]

                    def then(ins):
                        n[0] += 1
                        ins.then_inc(win_step, 1)
                        dve.wait_ge(win_step, n[0])

                    def norm(b):
                        dve.wait_ge(root_ready1, b + 1)
                        cols = rstd[:, b * BATCH:(b + 1) * BATCH]
                        nc.vector.reciprocal(cols, cols).then_inc(rstd_ready1, 1)
                        dve.wait_ge(rstd_ready1, b + 1)
                        for t in batches[b]:
                            last = normalise(H, t)
                        last.then_inc(norm_ready, 1)

                    windows(then)
                    for t in range(NT):
                        dve.wait_ge(node_done, t + 1)
                        if t >= 2:
                            dve.wait_ge(sig_ready, t - 1)
                        nc.vector.tensor_tensor(pre[:, t % 2, :], node_ps[:, t % BANKS, 0:PRE], sc[:, t, :],
                                                ALU.add).then_inc(pre_ready, 1)
                        dve.wait_ge(pre_ready, t + 1)
                        dve.wait_ge(sig_ready, t + 1)
                        nc.vector.scalar_tensor_tensor(out=val[:, t % 2, 0:S_CH], in0=pre[:, t % 2, 0:S_CH],
                                                       scalar=a_col[:, t:t + 1], in1=sig[:, t % 2, 0:S_CH],
                                                       op0=ALU.mult, op1=ALU.mult)
                        nc.vector.scalar_tensor_tensor(
                            out=val[:, t % 2, S_CH:D].rearrange("p (c i) -> p c i", i=3),
                            in0=pre[:, t % 2, S_OUT:PRE].rearrange("p (c i) -> p c i", i=3), scalar=a_col[:, t:t + 1],
                            in1=sig[:, t % 2, S_CH:S_OUT].unsqueeze(2).to_broadcast([P, V_CH, 3]),
                            op0=ALU.mult, op1=ALU.mult).then_inc(val_ready, 1)
                        dve.wait_ge(val_ready, t + 1)
                        nc.vector.tensor_tensor(X[:, t, :], X[:, t, :], val[:, t % 2, :], ALU.add).then_inc(x_ready, 1)
                        b, at = divmod(t, BATCH)
                        if at == BATCH - 1:
                            dve.wait_ge(x_ready, t + 1)
                            spread(dve, batches[b], b, stats_step1, var_ready1)
                        if at == 2 and b >= 1:
                            norm(b - 1)
                    norm(len(batches) - 1)

                @block.scalar
                def _(act):
                    def finish(b):
                        act.wait_ge(norm_ready, b + 1)
                        rows = H[:, b * BATCH:(b + 1) * BATCH, :]
                        nc.scalar.activation(rows, rows, ACT.Relu).then_inc(h1_ready, 1)

                    for t in range(NT):
                        act.wait_ge(pre_ready, t + 1)
                        if t >= 2:
                            act.wait_ge(val_ready, t - 1)
                        nc.scalar.activation(sig[:, t % 2, :], pre[:, t % 2, 0:S_OUT], ACT.Sigmoid,
                                             scale=a_col[:, t:t + 1]).then_inc(sig_ready, 1)
                        b, at = divmod(t, BATCH)
                        if b >= 1 and at == 0:
                            act.wait_ge(var_ready1, b)
                            root(batches[b - 1], root_ready1)
                        if b >= 1 and at == 3:
                            finish(b - 1)
                    act.wait_ge(var_ready1, len(batches))
                    root(batches[-1], root_ready1)
                    finish(len(batches) - 1)

                @block.gpsimd
                def _(pool):
                    for t in range(NT):
                        pool.wait_ge(node_done, t + 1)
                        nc.gpsimd.memset(acc[:, :, t * P:(t + 1) * P], 0.0).then_inc(cleared, 1)
                        b, at = divmod(t, BATCH)
                        if b >= 1 and at == BATCH - 1:
                            pool.wait_ge(h1_ready, b)
                            rows = slice((b - 1) * BATCH, b * BATCH)
                            nc.gpsimd.tensor_tensor(X[:, rows, :], X[:, rows, :], H[:, rows, :], ALU.add).then_inc(added, 1)
                    nc.gpsimd.memset(acc[:, :, NPAD:ACC_W], 0.0).then_inc(cleared, 1)
                    pool.wait_ge(h1_ready, len(batches))
                    rows = slice(NT - BATCH, NT)
                    nc.gpsimd.tensor_tensor(X[:, rows, :], X[:, rows, :], H[:, rows, :], ALU.add).then_inc(added, 1)
                    pool.wait_ge(cleared, NT + 1)

                @block.sync
                def _(sp):
                    for b in range(len(batches)):
                        rows = slice(b * BATCH, (b + 1) * BATCH)
                        sp.wait_ge(h1_ready, b + 1)
                        sp.dma_start(table_v[1][:, rows, :], H[:, rows, :]).then_inc(table_out, 16)
                    sp.wait_ge(table_out, 16 * len(batches))

        edge_passes(1)

        with ExitStack() as st:
            node_ps = st.enter_context(nc.psum_tensor("node_ps1", [P, 2, 512], F32))
            big1_sb = sb("big1_sb", [P, PLANES, D], scope=st)
            big1_in = sem("big1_in")
            node_done = sem("node1_done")
            y_ready = sem("y_ready")
            y_out = sem("y_out")
            with nc.Block() as block:
                @block.tensor
                def _(pe):
                    pe.wait_ge(big1_in, 16)
                    for t in range(NT):
                        if t >= 2:
                            pe.wait_ge(y_ready, t - 1)
                        for m in range(PLANES):
                            last = nc.tensor.matmul(node_ps[:, t % 2, 0:D], acc[:, m, t * P:(t + 1) * P],
                                                    big1_sb[:, m, :], start=(m == 0), stop=(m == PLANES - 1))
                        last.then_inc(node_done, 1)

                @block.vector
                def _(dve):
                    for t in range(NT):
                        dve.wait_ge(node_done, t + 1)
                        nc.vector.scalar_tensor_tensor(out=X[:, t, :], in0=node_ps[:, t % 2, 0:D], scalar=0.0,
                                                       in1=X[:, t, :], op0=ALU.max, op1=ALU.add).then_inc(y_ready, 1)

                @block.sync
                def _(sp):
                    sp.dma_start(big1_sb[:], big1_kept).then_inc(big1_in, 16)
                    for t in range(0, NT, 5):
                        sp.wait_ge(y_ready, t + 5)
                        sp.dma_start(out_v[:, t:t + 5, :], X[:, t:t + 5, :]).then_inc(y_out, 16)
                    sp.wait_ge(y_out, 16 * (NT // 5))


def _place_vec(to, w, rows, cols, ri, ci):
    n, m = w.shape
    to[rows + ri:rows + 3 * n:3, cols + ci:cols + 3 * m:3] = w


def _layer0_planes(ws, wv, sign):
    full = np.zeros((4, MSG, PRE), np.float32)
    full[0, C_W1:C_W1 + S_CH, 0:S_OUT] = ws[0:S_CH]
    for k in range(1, 4):
        full[k, C_W4 + k - 1:C_W4 + VC:3, 0:S_OUT] = ws[S_CH:]
    for i in range(3):
        a, b = (i + 1) % 3, (i + 2) % 3
        full[i + 1, C_W2:C_W2 + S_CH, S_OUT + i:PRE:3] = wv[0:64]
        full[0, C_W3 + i:C_W3 + VC:3, S_OUT + i:PRE:3] = wv[64:96]
        full[b + 1, C_W5 + a:C_W5 + VC:3, S_OUT + i:PRE:3] = wv[96:128]
        low = full[a + 1, C_W5 + b:C_W5 + VC:3, S_OUT + i:PRE:3]
        low[...] = wv[96:128]
        if sign:
            low *= -1
    planes = np.zeros((PLANES, P, PRE), np.float32)
    for k in range(4):
        rows = full[k, C_W4 if k else C_W1:][0:HIGH_N]
        planes[k] = rows[0:P]
        planes[4 + k] = rows[P:]
    return np.ascontiguousarray(planes.transpose(1, 0, 2))


def _layer1_pair(w1, w2, w3, w4, w5, sign):
    full = np.zeros((4, D, D), np.float32)
    full[0, 0:S_CH, 0:S_CH] = w1
    for i in range(3):
        a, b = (i + 1) % 3, (i + 2) % 3
        full[i + 1, S_CH + i:D:3, 0:S_CH] = w2
        full[i + 1, 0:S_CH, S_CH + i:D:3] = w3
        full[0, S_CH + i:D:3, S_CH + i:D:3] = w4
        full[b + 1, S_CH + a:D:3, S_CH + i:D:3] = w5
        low = full[a + 1, S_CH + b:D:3, S_CH + i:D:3]
        low[...] = w5
        if sign:
            low *= -1
    planes = np.zeros((2, 4, 2, P, P), np.float32)
    for k in range(4):
        t = np.zeros((2 * P, D), np.float32)
        t[0:D] = full[k].T
        for h in range(2):
            planes[0, k, h] = t[h * P:(h + 1) * P, 0:P]
            planes[1, k, h, :, 2 * P - D:] = t[h * P:(h + 1) * P, P:D]
    return np.ascontiguousarray(planes.reshape(2 * PLANES, P, P).transpose(1, 0, 2))


def _block_rows(full, overlap):
    n = full.shape[1]
    c = np.zeros((P, 2, n), np.float32)
    c[:, 0] = full[0:P]
    if overlap:
        c[2 * P - D:, 1] = full[P:D]
    else:
        c[0:D - P, 1] = full[P:D]
    return c


def _square(s, v):
    full = np.zeros((D, s.shape[1] + 3 * v.shape[1]), np.float32)
    full[0:S_CH, 0:s.shape[1]] = s
    for i in range(3):
        full[S_CH + i:D:3, s.shape[1] + i::3] = v
    return full


def _ones(value, *shape):
    return np.full(shape, value, np.float32)


def kernel(x, src, dst, edge_attr_4, edge_attr_64, node_vec1, L0_gnn_lin1_ws, L0_gnn_lin1_wv, L0_gnn_fc_w1,
           L0_gnn_fc_w2, L0_gnn_sc_ws, L0_gnn_sc_wv, L0_gnn_lin2_ws, L0_gnn_lin2_wv, L1_gnn_W1, L1_gnn_W2,
           L1_gnn_W3, L1_gnn_W4, L1_gnn_W5, L1_gnn_Ws, L1_gnn_Wv):
    import concourse.bacc as bacc
    from concourse.bass_utils import run_bass_kernel_spmd

    A = lambda v: np.asarray(v)

    def pad(v, n, mode="constant"):
        v = A(v)
        return np.pad(v, [(0, n - v.shape[0])] + [(0, 0)] * (v.ndim - 1), mode=mode)

    by_edge = lambda v: np.ascontiguousarray(np.moveaxis(v.reshape((GROUPS * TILES, P) + v.shape[1:]), 0, 1))
    order = lambda v: np.ascontiguousarray(v.reshape((GROUPS, 2, 2, P) + v.shape[1:]).swapaxes(1, 2).reshape(v.shape))
    e_src = order(pad(src, E_PAD))
    e_dst = order(pad(dst, E_PAD, "edge"))
    e_sh = order(pad(edge_attr_4, E_PAD))
    feat = pad(edge_attr_64, E_PAD).reshape(GROUPS, 2, GROUP // 2, S_CH).transpose(0, 1, 3, 2).reshape(GROUPS, P, GROUP // 2)

    f = float
    lin_sc = np.concatenate([_square(A(L0_gnn_lin1_ws), A(L0_gnn_lin1_wv)), _square(A(L0_gnn_sc_ws), A(L0_gnn_sc_wv))], 1)
    i_s, i_v = f(S_CH) ** -0.5, f(V_CH) ** -0.5
    lin_k = np.concatenate([_square(_ones(i_s, S_CH, S_CH), _ones(i_v, V_CH, V_CH)),
                            _square(_ones(i_s, S_CH, S_OUT), _ones(i_v, V_CH, V_CH))], 1)
    fc1 = np.zeros((P, P), np.float32)
    fc2 = np.zeros((P, 2 * W_N), np.float32)
    for h in range(2):
        fc1[h * 64:(h + 1) * 64, h * 64:(h + 1) * 64] = A(L0_gnn_fc_w1)
        fc2[h * 64:(h + 1) * 64, h * W_N:(h + 1) * W_N] = A(L0_gnn_fc_w2)
    k_s = 64.0 ** -0.5 * 16.0 ** -0.5 * 96.0 ** -0.5
    k_v = 64.0 ** -0.5 * 16.0 ** -0.5 * 128.0 ** -0.5
    ks = np.concatenate([_ones(k_s, 64, 96), _ones(k_s * 3.0 ** -0.5, 32, 96)])
    kv = np.concatenate([_ones(k_v, 96, 32), _ones(k_v * 2.0 ** -0.5, 32, 32)])
    c0, c1 = (S_CH + V_CH) ** -0.5, (3.0 / (S_CH + 2 * V_CH)) ** 0.5
    inv3, inv6 = 3.0 ** -0.5, 6.0 ** -0.5

    arrays = {
        "x": pad(x, NPAD),
        "node_vec": np.ascontiguousarray(pad(node_vec1, NPAD).reshape(NT, P).T),
        "src_idx": np.ascontiguousarray(e_src.reshape(GROUPS // 2, 2 * TILES, P).transpose(0, 2, 1)),
        "dst_idx": by_edge(e_dst),
        "edge_sh": by_edge(e_sh),
        "edge_feat": np.ascontiguousarray(feat),
        "ident": np.eye(P, dtype=np.float32),
        "iota": np.tile(np.arange(WIN, dtype=np.float32), (P, 1)),
        "lin_sc": _block_rows(lin_sc, True),
        "lin_sc_scale": _block_rows(lin_k, True),
        "fc1": fc1,
        "fc2": fc2,
        "big0": _layer0_planes(A(L0_gnn_lin2_ws), A(L0_gnn_lin2_wv), False),
        "big0_scale": _layer0_planes(ks, kv, True),
        "l1_pair": _layer1_pair(A(L1_gnn_W1), A(L1_gnn_W2), A(L1_gnn_W3), A(L1_gnn_W4), A(L1_gnn_W5), False),
        "l1_pair_scale": _layer1_pair(_ones(c0, 64, 64), _ones(c0 * inv3, 32, 64), _ones(c1 * inv3, 64, 32),
                                      _ones(c1 * inv3, 32, 32), _ones(c1 * inv6, 32, 32), True),
        "l1_out": _block_rows(_square(A(L1_gnn_Ws), A(L1_gnn_Wv)), False),
        "l1_out_scale": _block_rows(_square(_ones(i_s, 64, 64), _ones(i_v, 32, 32)), False),
    }
    nc = bacc.Bacc("TRN2", target_bir_lowering=False, num_devices=1)
    args = [nc.dram_tensor(n + "_dram", v.shape, mybir.dt.from_np(v.dtype), kind="ExternalInput").ap()
            for n, v in arrays.items()]
    out = nc.dram_tensor("out_dram", (NPAD, D), F32, kind="ExternalOutput").ap()
    build(nc, *args, out)
    r = run_bass_kernel_spmd(nc, [{n + "_dram": v for n, v in arrays.items()}], core_ids=[0])
    return r.results[0]["out_dram"][0:N]
```

```python
import numpy as np
from contextlib import ExitStack

import concourse.bass as bass
from concourse import mybir

F32 = mybir.dt.float32
I32 = mybir.dt.int32
ALU = mybir.AluOpType
ACT = mybir.ActivationFunctionType
AXX = mybir.AxisListType.X
RMAX = bass.bass_isa.ReduceOp.max

P = 128
N = 3125
E = 103125
NT = -(-N // P)
NPAD = NT * P
S_CH, V_CH = 64, 32
VC = 3 * V_CH
D = S_CH + VC
W_N = 2 * S_CH + 3 * V_CH
S_OUT = 96
PRE = S_OUT + VC
MSG = 2 * S_CH + 3 * VC
TILES = 4
GROUP = TILES * P
UNROLL = 4
GROUPS = -(-E // GROUP)
ITERS = -(-GROUPS // UNROLL)
LAST = GROUPS - (ITERS - 1) * UNROLL
SLOTS = ITERS * UNROLL
E_PAD = SLOTS * GROUP
WIN = 32
ACC_W = NPAD + WIN
EPS = 1e-5

C_W1, C_W3, C_W4, C_W5, C_W2 = 0, S_CH, S_CH + VC, S_CH + 2 * VC, S_CH + 3 * VC
SUM_N = (MSG - C_W4, D)
PLANES = tuple(n // WIN for n in SUM_N)
S_ALL, V_ALL = S_OUT + S_CH, 2 * VC
REACH = [(0, P), (0, P), (0, PRE)] + [(PRE - P, PRE)] * 5
assert S_OUT == VC
BATCH = 5
ROOTS = 3


def build(nc, x, node_vec, src_idx, dst_idx, edge_sh, edge_feat, ident, iota, lin_sc, lin_sc_scale,
          fc1, fc2, big0, big0_scale, l1_pair, l1_pair_scale, l1_out, l1_out_scale, out):
    table = [nc.dram_tensor(f"node_table_{l}", (NPAD, D), F32, kind="Internal").ap() for l in range(2)]
    x_v = x.rearrange("(n p) c -> p n c", p=P)
    out_v = out.rearrange("(n p) c -> p n c", p=P)
    table_v = [t.rearrange("(n p) c -> p n c", p=P) for t in table]

    ctx = ExitStack()
    with ctx:
        def sb(name, shape, dt=F32, scope=ctx):
            return scope.enter_context(nc.sbuf_tensor(name, shape, dt))

        def sem(name):
            return ctx.enter_context(nc.semaphore(name))

        acc = sb("acc", [P, PLANES[0], ACC_W])
        X = sb("X", [P, NT, D])
        sc = sb("sc", [P, NT, PRE])
        a_col = sb("a_col", [P, NT])
        dst = sb("dst", [P, SLOTS * TILES], I32)
        rel = sb("rel", [P, SLOTS * TILES])
        sh = sb("sh", [P, SLOTS * TILES, 4])
        first = sb("first", [P, SLOTS])
        place = sb("place", [1, SLOTS])
        place_i = sb("place_i", [1, SLOTS], I32)
        turns_f = sb("turns_f", [1, 1])
        turns_i = sb("turns_i", [1, 3], I32)
        ident_sb = sb("ident_sb", [P, P])
        iota_sb = sb("iota_sb", [P, WIN])
        fc1_sb = sb("fc1_sb", [P, P])
        fc2_sb = sb("fc2_sb", [P, 2 * W_N])
        big1_sb = sb("big1_sb", [P, PLANES[1], D])
        big0_sb = sb("big0_sb", [P, PLANES[0], PRE])
        stats = sb("stats", [P, NT, 6])
        mean_var = sb("mean_var", [P, NT, 2])
        rstd = sb("rstd", [P, NT])
        eps_col = sb("eps_col", [P, 1])

        edge_idx = [sb(f"idx{l}", [P, 2, 2 * TILES], I32) for l in range(2)]
        edge_idx_in = [[sem(f"l{l}_idx_in{h}") for h in range(2)] for l in range(2)]
        feat = sb("feat", [P, UNROLL, GROUP // 2])
        feat_in = [sem(f"feat_in{u}") for u in range(UNROLL)]

        def load_idx(sp, layer, pair, h):
            sp.dma_start(edge_idx[layer][:, h, :], src_idx[bass.ds(pair, 1), :, :].rearrange("a p t -> (a p) t")).then_inc(edge_idx_in[layer][h], 16)

        def load_feat(sp, group, u):
            sp.dma_start(feat[:, u, :], edge_feat[bass.ds(group, 1), :, :].rearrange("a p c -> (a p) c")).then_inc(feat_in[u], 16)

        def spread(dve, tiles, n, done, ready):
            for t in tiles:
                last = nc.vector.bn_stats(stats[:, t, :], X[:, t, :])
            last.then_inc(done, 1)
            dve.wait_ge(done, n + 1)
            aggregated(tiles, ready)

        def aggregated(tiles, ready):
            for t in tiles:
                last = nc.vector.bn_aggr(mean_var[:, t, :], stats[:, t, :])
            last.then_inc(ready, 1)

        def root(tiles, ready):
            nc.scalar.activation(rstd[:, tiles[0]:tiles[-1] + 1], mean_var[:, tiles[0]:tiles[-1] + 1, 1], ACT.Sqrt,
                                 bias=eps_col[:, 0:1]).then_inc(ready, 1)

        def normalise(H, t):
            return nc.vector.tensor_scalar(H[:, t, :], X[:, t, :], mean_var[:, t, 0:1], rstd[:, t:t + 1],
                                           ALU.subtract, ALU.mult)

        def windows(then):
            wide = [P, SLOTS, TILES]
            then(nc.vector.tensor_tensor(rel[:].rearrange("p (g t) -> p g t", t=TILES),
                                         dst[:].rearrange("p (g t) -> p g t", t=TILES),
                                         first[:].unsqueeze(2).to_broadcast(wide), ALU.subtract))
            then(nc.vector.tensor_copy(place[:], first[0:1, :]))
            then(nc.vector.tensor_copy(place_i[:], place[:]))

        with ExitStack() as st:
            H = sb("h0", [P, NT, D], scope=st)
            hT = sb("hT", [P, 2, 2, P], scope=st)
            lin = sb("lin", [P, S_ALL + V_ALL], scope=st)
            lin_k = sb("lin_k", [P, S_ALL + V_ALL], scope=st)
            wout = sb("wout", [P, 2, D], scope=st)
            wout_k = sb("wout_k", [P, 2, D], scope=st)
            least = sb("least", [P, 2, SLOTS], scope=st)
            both = sb("both", [P, 2, SLOTS], scope=st)
            spare = acc[:, PLANES[0] - 2:, :].rearrange("p a n -> p (a n)")
            n_pair, n_big = 2 * PLANES[1] * P, PLANES[0] * PRE
            pair = spare[:, 0:n_pair].rearrange("p (m n) -> p m n", n=P)
            pair_k = spare[:, n_pair:2 * n_pair].rearrange("p (m n) -> p m n", n=P)
            big_k = spare[:, 2 * n_pair:2 * n_pair + n_big].rearrange("p (c n) -> p c n", c=PLANES[0])
            span = spare[:, 2 * n_pair + n_big:2 * n_pair + n_big + SLOTS]
            tp = st.enter_context(nc.psum_tensor("tp", [P, 2, 2, 256], F32))
            mm = st.enter_context(nc.psum_tensor("mm", [P, 4, 512], F32))
            cp = st.enter_context(nc.psum_tensor("cp", [P, 2, 512], F32))
            BANKS, LAG, MID = 4, 3, 10

            x_in = [sem(f"x_in{b}") for b in range(NT // BATCH)]
            dst_in = sem("dst_in")
            lin_in = sem("lin_in")
            w_in = sem("w_in")
            edges_in = sem("edges_in")
            eps_set = sem("eps_set")
            stats_step = sem("stats_step")
            var_ready = sem("var_ready")
            root_ready = sem("root_ready")
            rstd_ready = sem("rstd_ready")
            h0_ready = sem("h0_ready")
            lin_ready = sem("lin_ready")
            least_ready = sem("least_ready")
            both_ready = sem("both_ready")
            weights_ready = sem("weights_ready")
            big0_ready = sem("big0_ready")
            hT_turned = sem("hT_turned")
            hT_ready = sem("hT_ready")
            lin_done = sem("lin_done")
            rows_ready = sem("rows_ready")
            sc_ready = sem("sc_ready")
            rows_out = sem("rows_out")
            comp_done = sem("comp_done")
            comp_copied = sem("comp_copied")
            windows_set = sem("windows_set")
            acc_clear = sem("acc_clear")
            setup_step = sem("setup_step")
            batches = [range(b, b + BATCH) for b in range(0, NT, BATCH)]

            with nc.Block() as block:
                @block.sync
                def _(sp):
                    for b, tiles in enumerate(batches):
                        sp.dma_start(X[:, tiles[0]:tiles[-1] + 1, :], x_v[:, tiles[0]:tiles[-1] + 1, :]).then_inc(x_in[b], 16)
                        if b == 0:
                            sp.dma_start(a_col[:], node_vec).then_inc(lin_in, 16)
                    sp.dma_start(dst[:], dst_idx).then_inc(dst_in, 16)
                    sp.dma_start(pair, l1_pair).then_inc(w_in, 16)
                    sp.dma_start(pair_k, l1_pair_scale).then_inc(w_in, 16)
                    sp.dma_start(wout[:], l1_out).then_inc(w_in, 16)
                    sp.dma_start(wout_k[:], l1_out_scale).then_inc(w_in, 16)
                    sp.dma_start(big0_sb[:], big0).then_inc(w_in, 16)
                    sp.dma_start(big_k, big0_scale).then_inc(w_in, 16)
                    sp.dma_start(iota_sb[:], iota).then_inc(edges_in, 16)
                    sp.dma_start(fc1_sb[:], fc1).then_inc(edges_in, 16)
                    sp.dma_start(fc2_sb[:], fc2).then_inc(edges_in, 16)
                    sp.dma_start(sh[:], edge_sh).then_inc(edges_in, 16)
                    for h in range(2):
                        load_idx(sp, 0, h, h)
                    for u in range(UNROLL):
                        load_feat(sp, u, u)
                    for b, tiles in enumerate(batches):
                        at = slice(tiles[0], tiles[-1] + 1)
                        sp.wait_ge(rows_ready, tiles[-1] + 1)
                        sp.dma_start(table_v[0][:, at, :], H[:, at, :]).then_inc(rows_out, 16)
                    sp.wait_ge(rows_out, 16 * len(batches))
                    sp.wait_ge(edges_in, 64)

                @block.gpsimd
                def _(pool):
                    nc.gpsimd.memset(acc[:, 0:PLANES[0] - 2, :], 0.0).then_inc(acc_clear, 1)
                    pool.wait_ge(w_in, 6 * 16)
                    nc.gpsimd.tensor_tensor(big0_sb[:], big0_sb[:], big_k, ALU.mult).then_inc(big0_ready, 1)
                    pool.wait_ge(least_ready, 1)
                    nc.gpsimd.partition_all_reduce(both[:].rearrange("p a g -> p (a g)"),
                                                   least[:].rearrange("p a g -> p (a g)"), P, RMAX).then_inc(both_ready, 1)
                    pool.wait_ge(comp_done, PLANES[1])
                    pool.wait_ge(windows_set, 1)
                    pool.wait_ge(big0_ready, 1)
                    nc.gpsimd.memset(acc[:, PLANES[0] - 2:, :], 0.0).then_inc(acc_clear, 1)
                    pool.wait_ge(acc_clear, 2)

                @block.vector
                def _(dve):
                    n = [0]

                    def then(ins):
                        n[0] += 1
                        ins.then_inc(setup_step, 1)
                        dve.wait_ge(setup_step, n[0])

                    nc.vector.memset(eps_col[:], EPS).then_inc(eps_set, 1)
                    def spread_batch(b):
                        dve.wait_ge(x_in[b], 16)
                        spread(dve, batches[b], b, stats_step, var_ready)

                    spread_batch(0)
                    spread_batch(1)
                    dve.wait_ge(lin_in, 64)
                    nc.vector.tensor_tensor(lin[:], lin[:], lin_k[:], ALU.mult).then_inc(lin_ready, 1)
                    for t in range(NT + LAG):
                        if t < NT:
                            b, at = divmod(t, BATCH)
                            if at == 0:
                                dve.wait_ge(root_ready, b + 1)
                                cols = rstd[:, t:t + BATCH]
                                nc.vector.reciprocal(cols, cols).then_inc(rstd_ready, 1)
                                dve.wait_ge(rstd_ready, b + 1)
                            normalise(H, t).then_inc(h0_ready, 1)
                            if at == 1 and b + 2 < len(batches):
                                spread_batch(b + 2)
                        if t >= LAG:
                            u = t - LAG
                            dve.wait_ge(lin_done, u + 1)
                            got = mm[:, u % BANKS, :]
                            nc.vector.tensor_scalar(H[:, u, :], got[:, S_OUT:S_OUT + D], a_col[:, u:u + 1],
                                                    None, ALU.mult).then_inc(rows_ready, 1)
                        if t == MID:
                            dve.wait_ge(w_in, 6 * 16)
                            nc.vector.tensor_tensor(pair, pair, pair_k, ALU.mult)
                            nc.vector.tensor_tensor(wout[:], wout[:], wout_k[:], ALU.mult).then_inc(weights_ready, 1)
                        if t == MID + 1:
                            dve.wait_ge(dst_in, 16)
                            by_group = dst[:].rearrange("p (g t) -> p g t", t=TILES)
                            then(nc.vector.tensor_reduce(least[:, 0, :], by_group, AXX, ALU.min))
                            then(nc.vector.tensor_scalar(least[:, 0, :], least[:, 0, :], -1.0, None, ALU.mult))
                            nc.vector.tensor_reduce(least[:, 1, :], by_group, AXX, ALU.max).then_inc(least_ready, 1)
                        if t == MID + 7:
                            dve.wait_ge(both_ready, 1)
                            then(nc.vector.tensor_scalar(first[:], both[:, 0, :], -1.0, None, ALU.mult))
                            then(nc.vector.tensor_tensor(span, both[:, 0, :], both[:, 1, :], ALU.add))
                            then(nc.vector.tensor_reduce(turns_f[:], span[0:1, :], AXX, ALU.max))
                            then(nc.vector.tensor_copy(turns_i[:, 0:1], turns_f[:]))
                            then(nc.vector.tensor_scalar(turns_i[:, 1:2], turns_i[:, 0:1], WIN.bit_length() - 1, None,
                                                         ALU.arith_shift_right))
                            then(nc.vector.tensor_scalar(turns_i[:, 2:3], turns_i[:, 1:2], float(ITERS), float(ITERS),
                                                         ALU.mult, ALU.add))
                        if t == MID + 9:
                            windows(then)
                            nc.vector.tensor_copy(place_i[:], place[:]).then_inc(windows_set, 1)

                @block.scalar
                def _(act):
                    act.dma_start(lin[:], lin_sc).then_inc(lin_in, 16)
                    act.dma_start(lin_k[:], lin_sc_scale).then_inc(lin_in, 16)
                    act.dma_start(ident_sb[:], ident).then_inc(lin_in, 16)
                    act.wait_ge(eps_set, 1)

                    def root_batch(b):
                        act.wait_ge(var_ready, b + 1)
                        root(batches[b], root_ready)

                    root_batch(0)
                    root_batch(1)
                    for t in range(NT + LAG):
                        if t < NT:
                            act.wait_ge(hT_turned, t + 1)
                            if t >= 2:
                                act.wait_ge(lin_done, t - 1)
                            nc.scalar.activation(hT[:, t % 2, :, :], tp[:, t % 2, :, 0:P], ACT.Relu).then_inc(hT_ready, 1)
                        if t >= LAG:
                            u = t - LAG
                            act.wait_ge(rows_ready, u + 1)
                            got = mm[:, u % BANKS, 0:2 * (S_OUT + D)].rearrange("p (a c) -> p a c", a=2)[:, :, 0:S_OUT]
                            nc.scalar.activation(sc[:, u, :].rearrange("p (a c) -> p a c", a=2), got,
                                                 ACT.Copy).then_inc(sc_ready, 1)
                        if t % BATCH == 3 and t // BATCH + 2 < len(batches):
                            root_batch(t // BATCH + 2)
                        if t == MID:
                            for m in range(PLANES[1]):
                                act.wait_ge(comp_done, m + 1)
                                nc.scalar.activation(big1_sb[:, m, :], cp[:, m % 2, 0:D], ACT.Copy).then_inc(comp_copied, 1)

                @block.tensor
                def _(pe):
                    pe.wait_ge(lin_ready, 1)
                    for t in range(NT + 1):
                        if t < NT:
                            pe.wait_ge(h0_ready, t + 1)
                            if t >= 2:
                                pe.wait_ge(hT_ready, t - 1)
                            nc.tensor.transpose(tp[:, t % 2, 0, 0:P], H[:, t, 0:P], ident_sb[:])
                            nc.tensor.transpose(tp[:, t % 2, 1, 0:P], H[:, t, D - P:D], ident_sb[:]).then_inc(hT_turned, 1)
                        if t >= 1:
                            u = t - 1
                            pe.wait_ge(hT_ready, u + 1)
                            if u >= BANKS:
                                pe.wait_ge(rows_ready, u - BANKS + 1)
                                pe.wait_ge(sc_ready, u - BANKS + 1)
                            for c, cols in enumerate((slice(0, S_ALL), slice(S_ALL, S_ALL + V_ALL))):
                                last = nc.tensor.matmul(mm[:, u % BANKS, cols], hT[:, u % 2, c, :], lin[:, cols],
                                                        start=True, stop=True)
                            last.then_inc(lin_done, 1)
                        if t == MID:
                            pe.wait_ge(weights_ready, 1)
                            for m in range(PLANES[1]):
                                if m >= 2:
                                    pe.wait_ge(comp_copied, m - 1)
                                for c in range(2):
                                    last = nc.tensor.matmul(cp[:, m % 2, 0:D], pair[:, 2 * m + c, :], wout[:, c, :],
                                                            start=(c == 0), stop=(c == 1))
                                last.then_inc(comp_done, 1)

        def edge_passes(layer):
            L = f"l{layer}_"
            own_weights = layer == 0
            width, planes = SUM_N[layer], PLANES[layer]
            with ExitStack() as st:
                idx = edge_idx[layer]
                g = sb(L + "g", [P, UNROLL, TILES, D], scope=st)
                hot = sb(L + "hot", [P, 2, TILES, WIN], scope=st)
                sel = sb(L + "sel", [P, 2, TILES, 4 * WIN], scope=st)
                turned = sb(L + "turned", [P, planes, WIN], scope=st)
                sums = st.enter_context(nc.psum_tensor(L + "sums", [P, 2, 512], F32))
                if own_weights:
                    hid = sb(L + "hid", [P, 2, GROUP // 2], scope=st)
                    prod = sb(L + "prod", [P, 2, TILES, MSG], scope=st)
                    hid_ps = st.enter_context(nc.psum_tensor(L + "hid_ps", [P, 512], F32))
                    w_ps = st.enter_context(nc.psum_tensor(L + "w_ps", [P, 4, 512], F32))

                idx_in = edge_idx_in[layer]
                gathered = [sem(L + f"gathered{u}") for u in range(UNROLL)]
                hid_done = sem(L + "hid_done")
                silu_done = sem(L + "silu_done")
                w_done = sem(L + "w_done")
                prod_done = sem(L + "prod_done")
                hot_done = sem(L + "hot_done")
                sel_done = sem(L + "sel_done")
                agg_done = sem(L + "agg_done")
                turn_done = sem(L + "turn_done")
                acc_done = sem(L + "acc_done")
                gather_begun = sem(L + "gather_begun")
                pass_left = sem(L + "pass_left")

                def passes(eng):
                    total = eng.value_load(turns_i[0:1, 2:3], min_val=ITERS, max_val=ITERS * (-(-N // WIN)))
                    return eng.Fori(0, total, ITERS)

                def pass_over(eng, q, *counts):
                    end = eng.snap(UNROLL * q + GROUPS)
                    eng.wait_ge(acc_done, end)
                    eng.sem_inc(pass_left, 1)
                    for done, per_group in counts:
                        eng.sem_inc(done, per_group * (SLOTS - GROUPS))

                def stages(eng, q, stage, last):
                    for s in range(UNROLL):
                        stage(q, 0, s, s)
                    with eng.Fori(1, ITERS - 1) as it:
                        f = eng.snap(q + it)
                        for o in range(UNROLL):
                            stage(f, it, o, None)
                    f = eng.snap(q + (ITERS - 1))
                    for s in range(SLOTS - UNROLL, last):
                        stage(f, ITERS - 1, s - (SLOTS - UNROLL), s)

                with nc.Block() as block:
                    @block.sync
                    def _(sp):
                        with passes(sp) as q:
                            with sp.Fori(0, ITERS - 1) as it:
                                f = sp.snap(q + it)
                                for u in range(UNROLL):
                                    group = sp.snap(UNROLL * it + (UNROLL + u))
                                    if u % 2:
                                        pair = sp.snap(2 * it + (2 + u // 2))
                                        rows = sp.snap(16 * TILES * f + 16 * TILES)
                                        sp.wait_ge(gathered[u - 1], rows)
                                        sp.wait_ge(gathered[u], rows)
                                        load_idx(sp, layer, pair, u // 2)
                                    if own_weights:
                                        used = sp.snap(UNROLL * f + (u + 1))
                                        sp.wait_ge(hid_done, used)
                                        load_feat(sp, group, u)
                            f = sp.snap(q + (ITERS - 1))
                            rows = sp.snap(16 * TILES * f + 16 * TILES)
                            landed = sp.snap(16 * f + 16)
                            for h in range(2):
                                for u in (2 * h, 2 * h + 1):
                                    sp.wait_ge(gathered[u], rows)
                                load_idx(sp, layer, h, h)
                            if own_weights:
                                for u in range(UNROLL):
                                    if u < LAST:
                                        used = sp.snap(UNROLL * f + (u + 1))
                                        sp.wait_ge(hid_done, used)
                                    else:
                                        sp.wait_ge(feat_in[u], landed)
                                    load_feat(sp, u, u)
                            pass_over(sp, q)
                            end = sp.snap(16 * f + 32)
                            for h in range(2):
                                sp.wait_ge(idx_in[h], end)
                            if own_weights:
                                for u in range(UNROLL):
                                    sp.wait_ge(feat_in[u], end)
                            sp.sem_inc(pass_left, 1)

                    @block.gpsimd
                    def _(pool):
                        def gather(f, u, full, rows=True):
                            used = pool.snap(2 * UNROLL * f + (2 * u + 2 - 2 * UNROLL)) if full else None
                            there = pool.snap(16 * f + 16)
                            if u % 2 == 0:
                                pool.wait_ge(idx_in[u // 2], there)
                            if full:
                                pool.wait_ge(prod_done if own_weights else agg_done, used)
                            if full or u % 2 == 0:
                                pool.sem_inc(gather_begun, 1)
                            if not rows:
                                nc.gpsimd.dma_start(g[0:1, u, 0, :], table[layer][0:1, :]).then_inc(gathered[u], 16 * TILES)
                                return
                            for j in range(TILES):
                                nc.gpsimd.indirect_dma_start(
                                    out=g[:, u, j, :], out_offset=None, in_=table[layer],
                                    in_offset=bass.IndirectOffsetOnAxis(ap=idx[:, u // 2, (u % 2) * TILES + j:(u % 2) * TILES + j + 1], axis=0),
                                ).then_inc(gathered[u], 16)

                        with passes(pool) as q:
                            for u in range(UNROLL):
                                gather(q, u, False)
                            with pool.Fori(1, ITERS - 1) as it:
                                f = pool.snap(q + it)
                                for u in range(UNROLL):
                                    gather(f, u, True)
                            f = pool.snap(q + (ITERS - 1))
                            for u in range(UNROLL):
                                gather(f, u, True, rows=u < LAST)
                            pass_over(pool, q)
                            end = pool.snap(16 * TILES * f + 16 * TILES)
                            for u in range(LAST, UNROLL):
                                pool.wait_ge(gathered[u], end)

                    @block.scalar
                    def _(act):
                        def silu(f, o, s):
                            act.wait_ge(hid_done, UNROLL * f + (o + 1))
                            if s is None or s >= 2:
                                act.wait_ge(w_done, 2 * UNROLL * f + (2 * o - 2))
                            nc.scalar.activation(hid[:, o % 2, :], hid_ps[:, 0:GROUP // 2], ACT.Silu,
                                                 scale=float(S_CH) ** -0.5).then_inc(silu_done, 1)

                        def stage(f, it, o, s):
                            if s == 0:
                                silu(f, 0, 0)
                            if s is None or s + 1 < GROUPS:
                                silu(f, o + 1, None if s is None else s + 1)

                        if own_weights:
                            with passes(act) as q:
                                stages(act, q, stage, GROUPS - 1)
                                pass_over(act, q, (silu_done, 1))

                    @block.vector
                    def _(dve):
                        def select(f, it, o, s):
                            if s is None or s >= 2:
                                dve.wait_ge(agg_done, 2 * UNROLL * f + (2 * o - 2))
                            at = bass.ds(UNROLL * TILES * it + TILES * o, TILES)
                            nc.vector.tensor_tensor(hot[:, o % 2, :, :], iota_sb[:].unsqueeze(1).to_broadcast([P, TILES, WIN]),
                                                    rel[:, at].unsqueeze(2).to_broadcast([P, TILES, WIN]),
                                                    ALU.is_equal).then_inc(hot_done, 1)
                            dve.wait_ge(hot_done, UNROLL * f + (o + 1))
                            nc.vector.tensor_tensor(sel[:, o % 2, :, :].rearrange("p t (k n) -> p t k n", k=4),
                                                    hot[:, o % 2, :, :].unsqueeze(2).to_broadcast([P, TILES, 4, WIN]),
                                                    sh[:, at, :].unsqueeze(3).to_broadcast([P, TILES, 4, WIN]),
                                                    ALU.mult).then_inc(sel_done, 1)

                        def products(f, o, h):
                            u = o % UNROLL
                            dve.wait_ge(w_done, 2 * UNROLL * f + (2 * o + h + 1))
                            if h == 0:
                                dve.wait_ge(gathered[u], 16 * TILES * f + 16 * TILES * (o // UNROLL + 1))
                            w = w_ps[:, o % 2 * 2 + h, 0:2 * W_N].rearrange("p (t c) -> p t c", t=2)
                            rows = g[:, u, 2 * h:2 * h + 2, :]
                            to = prod[:, o % 2, 2 * h:2 * h + 2, :]
                            s_cols = to[:, :, 0:S_CH]
                            both = bass.AP(s_cols.tensor, s_cols.offset,
                                           [*s_cols.ap[0:2], [C_W2 - C_W1, 2], s_cols.ap[2]])
                            for t in range(2):
                                nc.vector.tensor_tensor(
                                    to[:, t, C_W3:C_W2].rearrange("p (j c i) -> p j c i", j=3, i=3),
                                    w[:, t, 2 * S_CH:W_N].rearrange("p (j c) -> p j c", j=3).unsqueeze(3).to_broadcast([P, 3, V_CH, 3]),
                                    rows[:, t, S_CH:D].rearrange("p (c i) -> p c i", i=3).unsqueeze(1).to_broadcast([P, 3, V_CH, 3]),
                                    ALU.mult)
                            nc.vector.tensor_tensor(
                                both,
                                w[:, :, 0:2 * S_CH].rearrange("p t (j c) -> p t j c", j=2),
                                rows[:, :, 0:S_CH].unsqueeze(2).to_broadcast([P, 2, 2, S_CH]),
                                ALU.mult).then_inc(prod_done, 1)

                        def accumulate(f, it, o, s):
                            base = dve.value_load(place_i[0:1, bass.ds(UNROLL * it + o, 1)], min_val=0, max_val=NPAD)
                            dve.wait_ge(agg_done, 2 * UNROLL * f + (2 * o + 2))
                            if s != 0:
                                dve.wait_ge(acc_done, UNROLL * f + o)
                            nc.vector.transpose(turned[:].rearrange("p c n -> p (c n)"),
                                                sums[:, o % 2, 0:width]).then_inc(turn_done, 1)
                            dve.wait_ge(turn_done, UNROLL * f + (o + 1))
                            at = bass.ds(base, WIN)
                            nc.vector.tensor_tensor(acc[:, 0:planes, at], acc[:, 0:planes, at], turned[:],
                                                    ALU.add).then_inc(acc_done, 1)

                        def stage(f, it, o, s):
                            if s is None or s < GROUPS:
                                select(f, it, o, s)
                                if own_weights:
                                    products(f, o, 0)
                                    products(f, o, 1)
                            if s is None or s >= 2:
                                accumulate(f, it, o - 2, None if s is None else s - 2)

                        with passes(dve) as q:
                            stages(dve, q, stage, GROUPS + 2)
                            pass_over(dve, q, (hot_done, 1), (sel_done, 1), (turn_done, 1), (acc_done, 1),
                                      *(((prod_done, 2),) if own_weights else ()))
                            nc.vector.tensor_scalar(rel[:], rel[:], float(WIN), None, ALU.subtract)
                            nc.vector.tensor_scalar(place[:], place[:], float(WIN), float(NPAD), ALU.add, ALU.min)
                            dve.drain()
                            nc.vector.tensor_copy(place_i[:], place[:])
                            dve.drain()

                    @block.tensor
                    def _(pe):
                        def hidden(f, o, s):
                            pe.wait_ge(feat_in[o % UNROLL], 16 * f + 16 * (o // UNROLL + 1))
                            if s != 0:
                                pe.wait_ge(silu_done, UNROLL * f + o)
                            nc.tensor.matmul(hid_ps[:, 0:GROUP // 2], fc1_sb[:], feat[:, o % UNROLL, :],
                                             start=True, stop=True).then_inc(hid_done, 1)

                        def edge_weights(f, o, h, s):
                            if h == 0:
                                pe.wait_ge(silu_done, UNROLL * f + (o + 1))
                            if s is None or s >= 2:
                                pe.wait_ge(prod_done, 2 * UNROLL * f + (2 * o + h - 3))
                            nc.tensor.matmul(w_ps[:, o % 2 * 2 + h, 0:2 * W_N], hid[:, o % 2, h * P:(h + 1) * P], fc2_sb[:],
                                             start=True, stop=True).then_inc(w_done, 1)

                        def aggregate(f, o, h, s):
                            if own_weights:
                                pe.wait_ge(prod_done, 2 * UNROLL * f + (2 * o + h + 1))
                            if h == 0:
                                pe.wait_ge(sel_done, UNROLL * f + (o + 1))
                                if s is None or s >= 2:
                                    pe.wait_ge(turn_done, UNROLL * f + (o - 1))
                                if not own_weights:
                                    pe.wait_ge(gathered[o % UNROLL], 16 * TILES * f + 16 * TILES * (o // UNROLL + 1))
                            for j in (2 * h, 2 * h + 1):
                                first_last = dict(start=(j == 0), stop=(j == TILES - 1))
                                if own_weights:
                                    for k in range(4):
                                        c = C_W4 if k else C_W1
                                        at = slice(k * WIN, (k + 1) * WIN)
                                        last = nc.tensor.matmul(sums[at, o % 2, 0:width], sel[:, o % 2, j, at],
                                                                prod[:, o % 2, j, c:c + width],
                                                                tile_position=(0, k * WIN), **first_last)
                                else:
                                    last = nc.tensor.matmul(sums[:, o % 2, 0:D], sel[:, o % 2, j, :],
                                                            g[:, o % UNROLL, j, :], **first_last)
                            last.then_inc(agg_done, 1)

                        def stage(f, it, o, s):
                            before = None if s is None else s - 1
                            if own_weights:
                                if s == 0:
                                    hidden(f, 0, 0)
                                if s is None or s < GROUPS:
                                    edge_weights(f, o, 0, s)
                                    edge_weights(f, o, 1, s)
                                if s is None or s + 1 < GROUPS:
                                    hidden(f, o + 1, None if s is None else s + 1)
                                if s is None or 1 <= s <= GROUPS:
                                    aggregate(f, o - 1, 0, before)
                                    aggregate(f, o - 1, 1, before)
                            else:
                                if s is None or s < GROUPS:
                                    aggregate(f, o, 0, s)
                                    aggregate(f, o, 1, s)

                        with passes(pe) as q:
                            stages(pe, q, stage, GROUPS + 1 if own_weights else GROUPS)
                            pass_over(pe, q, (agg_done, 2),
                                      *(((hid_done, 1), (w_done, 2)) if own_weights else ()))

        edge_passes(0)

        with ExitStack() as st:
            H = sb("h1", [P, NT, D], scope=st)
            pre = sb("pre", [P, 2, PRE], scope=st)
            sig = sb("sig", [P, 2, S_OUT], scope=st)
            val = sb("val", [P, 2, D], scope=st)
            node_ps = st.enter_context(nc.psum_tensor("node_ps0", [P, 4, 512], F32))
            node_done = sem("node0_done")
            pre_ready = sem("pre_ready")
            sig_ready = sem("sig_ready")
            val_ready = sem("val_ready")
            x_ready = sem("x_ready")
            stats_step1 = sem("stats_step1")
            var_ready1 = sem("var_ready1")
            root_ready1 = sem("root_ready1")
            rstd_ready1 = sem("rstd_ready1")
            norm_ready = sem("norm_ready")
            h1_ready = sem("h1_ready")
            table_out = sem("table_out")
            cleared = sem("acc_cleared_again")
            win_step = sem("win_step")
            added = sem("added")
            BANKS = 4
            edges = [round(NT * b / ROOTS) for b in range(ROOTS + 1)]
            batches = [range(a, b) for a, b in zip(edges, edges[1:])]
            parts = [(batches[b][0], (batches[b][0] + batches[b][-1] + 1) // 2, batches[b][-1] + 1) for b in range(ROOTS)]
            parts = [[slice(a, b), slice(b, c)] for a, b, c in parts]

            with nc.Block() as block:
                @block.tensor
                def _(pe):
                    for t in range(NT):
                        if t >= BANKS:
                            pe.wait_ge(pre_ready, t - BANKS + 1)
                        for n, m in enumerate((2, 0, 1, 3, 4, 5, 6, 7)):
                            cols = slice(*REACH[m])
                            last = nc.tensor.matmul(node_ps[:, t % BANKS, cols], acc[:, m, t * P:(t + 1) * P],
                                                    big0_sb[:, m, cols], start=(n == 0), stop=(n == PLANES[0] - 1))
                        last.then_inc(node_done, 1)

                @block.vector
                def _(dve):
                    n = [0]

                    def then(ins):
                        n[0] += 1
                        ins.then_inc(win_step, 1)
                        dve.wait_ge(win_step, n[0])

                    def norm(b, c):
                        if c == 0:
                            dve.wait_ge(root_ready1, b + 1)
                            cols = rstd[:, batches[b][0]:batches[b][-1] + 1]
                            nc.vector.reciprocal(cols, cols).then_inc(rstd_ready1, 1)
                            dve.wait_ge(rstd_ready1, b + 1)
                        for t in range(parts[b][c].start, parts[b][c].stop):
                            last = normalise(H, t)
                        last.then_inc(norm_ready, 1)

                    windows(then)
                    for t in range(NT + 2):
                        if t < NT:
                            dve.wait_ge(node_done, t + 1)
                            if t >= 2:
                                dve.wait_ge(sig_ready, t - 1)
                            nc.vector.tensor_tensor(pre[:, t % 2, :], node_ps[:, t % BANKS, 0:PRE], sc[:, t, :],
                                                    ALU.add).then_inc(pre_ready, 1)
                        if 1 <= t <= NT:
                            u = t - 1
                            dve.wait_ge(pre_ready, u + 1)
                            dve.wait_ge(sig_ready, u + 1)
                            nc.vector.scalar_tensor_tensor(out=val[:, u % 2, 0:S_CH], in0=pre[:, u % 2, 0:S_CH],
                                                           scalar=a_col[:, u:u + 1], in1=sig[:, u % 2, 0:S_CH],
                                                           op0=ALU.mult, op1=ALU.mult)
                            nc.vector.scalar_tensor_tensor(
                                out=val[:, u % 2, S_CH:D].rearrange("p (c i) -> p c i", i=3),
                                in0=pre[:, u % 2, S_OUT:PRE].rearrange("p (c i) -> p c i", i=3), scalar=a_col[:, u:u + 1],
                                in1=sig[:, u % 2, S_CH:S_OUT].unsqueeze(2).to_broadcast([P, V_CH, 3]),
                                op0=ALU.mult, op1=ALU.mult).then_inc(val_ready, 1)
                            dve.wait_ge(val_ready, u + 1)
                            nc.vector.tensor_tensor(X[:, u, :], X[:, u, :], val[:, u % 2, :], ALU.add).then_inc(x_ready, 1)
                        if t >= 2:
                            u = t - 2
                            b = [u in tiles for tiles in batches].index(True)
                            at = u - batches[b][0]
                            dve.wait_ge(x_ready, u + 1)
                            nc.vector.bn_stats(stats[:, u, :], X[:, u, :]).then_inc(stats_step1, 1)
                            if u == batches[b][-1]:
                                dve.wait_ge(stats_step1, u + 1)
                                aggregated(batches[b], var_ready1)
                            if b >= 1 and at in (2, 4):
                                norm(b - 1, at // 2 - 1)
                    norm(ROOTS - 1, 0)
                    norm(ROOTS - 1, 1)
                    dve.wait_ge(h1_ready, 2 * ROOTS)
                    rows = parts[-1][1]
                    nc.vector.tensor_tensor(X[:, rows, :], X[:, rows, :], H[:, rows, :], ALU.add).then_inc(added, 1)

                @block.scalar
                def _(act):
                    def finish(b, c):
                        act.wait_ge(norm_ready, 2 * b + c + 1)
                        rows = H[:, parts[b][c], :]
                        nc.scalar.activation(rows, rows, ACT.Relu).then_inc(h1_ready, 1)

                    for t in range(NT):
                        act.wait_ge(pre_ready, t + 1)
                        if t >= 2:
                            act.wait_ge(val_ready, t - 1)
                        nc.scalar.activation(sig[:, t % 2, :], pre[:, t % 2, 0:S_OUT], ACT.Sigmoid,
                                             scale=a_col[:, t:t + 1]).then_inc(sig_ready, 1)
                        b = [t in tiles for tiles in batches].index(True)
                        at = t - batches[b][0]
                        if b >= 1 and at == 1:
                            act.wait_ge(var_ready1, b)
                            root(batches[b - 1], root_ready1)
                        if b >= 1 and at in (5, 7):
                            finish(b - 1, (at - 5) // 2)
                    act.wait_ge(var_ready1, ROOTS)
                    root(batches[-1], root_ready1)
                    finish(ROOTS - 1, 0)
                    finish(ROOTS - 1, 1)

                @block.gpsimd
                def _(pool):
                    for t in range(NT):
                        pool.wait_ge(node_done, t + 1)
                        nc.gpsimd.memset(acc[:, 0:PLANES[1], t * P:(t + 1) * P], 0.0).then_inc(cleared, 1)
                    nc.gpsimd.memset(acc[:, 0:PLANES[1], NPAD:ACC_W], 0.0).then_inc(cleared, 1)
                    for n in range(2 * ROOTS - 1):
                        pool.wait_ge(h1_ready, n + 1)
                        rows = parts[n // 2][n % 2]
                        nc.gpsimd.tensor_tensor(X[:, rows, :], X[:, rows, :], H[:, rows, :], ALU.add).then_inc(added, 1)
                    pool.wait_ge(cleared, NT + 1)

                @block.sync
                def _(sp):
                    for h in range(2):
                        load_idx(sp, 1, h, h)
                    for n in range(2 * ROOTS):
                        rows = parts[n // 2][n % 2]
                        sp.wait_ge(h1_ready, n + 1)
                        sp.dma_start(table_v[1][:, rows, :], H[:, rows, :]).then_inc(table_out, 16)
                    sp.wait_ge(table_out, 32 * ROOTS)

        edge_passes(1)

        with ExitStack() as st:
            node_ps = st.enter_context(nc.psum_tensor("node_ps1", [P, 2, 512], F32))
            node_done = sem("node1_done")
            y_ready = sem("y_ready")
            y_out = sem("y_out")
            with nc.Block() as block:
                @block.tensor
                def _(pe):
                    for t in range(NT):
                        if t >= 2:
                            pe.wait_ge(y_ready, t - 1)
                        for m in range(PLANES[1]):
                            last = nc.tensor.matmul(node_ps[:, t % 2, 0:D], acc[:, m, t * P:(t + 1) * P],
                                                    big1_sb[:, m, :], start=(m == 0), stop=(m == PLANES[1] - 1))
                        last.then_inc(node_done, 1)

                @block.vector
                def _(dve):
                    for t in range(NT):
                        dve.wait_ge(node_done, t + 1)
                        nc.vector.scalar_tensor_tensor(out=X[:, t, :], in0=node_ps[:, t % 2, 0:D], scalar=0.0,
                                                       in1=X[:, t, :], op0=ALU.max, op1=ALU.add).then_inc(y_ready, 1)

                @block.sync
                def _(sp):
                    for t in range(0, NT, 5):
                        sp.wait_ge(y_ready, t + 5)
                        sp.dma_start(out_v[:, t:t + 5, :], X[:, t:t + 5, :]).then_inc(y_out, 16)
                    sp.wait_ge(y_out, 16 * (NT // 5))


def _layer0_planes(ws, wv, sign):
    full = np.zeros((4, MSG, PRE), np.float32)
    full[0, C_W1:C_W1 + S_CH, 0:S_OUT] = ws[0:S_CH]
    for k in range(1, 4):
        full[k, C_W4 + k - 1:C_W4 + VC:3, 0:S_OUT] = ws[S_CH:]
    for i in range(3):
        a, b = (i + 1) % 3, (i + 2) % 3
        full[i + 1, C_W2:C_W2 + S_CH, S_OUT + i:PRE:3] = wv[0:64]
        full[0, C_W3 + i:C_W3 + VC:3, S_OUT + i:PRE:3] = wv[64:96]
        full[b + 1, C_W5 + a:C_W5 + VC:3, S_OUT + i:PRE:3] = wv[96:128]
        low = full[a + 1, C_W5 + b:C_W5 + VC:3, S_OUT + i:PRE:3]
        low[...] = wv[96:128]
        if sign:
            low *= -1
    planes = np.zeros((PLANES[0], 4, WIN, PRE), np.float32)
    for k in range(4):
        planes[:, k] = full[k, C_W4 if k else C_W1:][0:SUM_N[0]].reshape(PLANES[0], WIN, PRE)
    if not sign:
        for m, (a, b) in enumerate(REACH):
            assert not planes[m, 1:, :, 0:a].any() and not planes[m, 1:, :, b:].any()
    planes = planes.reshape(PLANES[0], P, PRE)
    return np.ascontiguousarray(planes.transpose(1, 0, 2))


def _layer1_pair(w1, w2, w3, w4, w5, sign):
    full = np.zeros((4, D, D), np.float32)
    full[0, 0:S_CH, 0:S_CH] = w1
    for i in range(3):
        a, b = (i + 1) % 3, (i + 2) % 3
        full[i + 1, S_CH + i:D:3, 0:S_CH] = w2
        full[i + 1, 0:S_CH, S_CH + i:D:3] = w3
        full[0, S_CH + i:D:3, S_CH + i:D:3] = w4
        full[b + 1, S_CH + a:D:3, S_CH + i:D:3] = w5
        low = full[a + 1, S_CH + b:D:3, S_CH + i:D:3]
        low[...] = w5
        if sign:
            low *= -1
    planes = np.zeros((PLANES[1], 2, P, 4, WIN), np.float32)
    for k in range(4):
        t = np.zeros((2 * P, D), np.float32)
        t[0:D] = full[k].T
        planes[:, :, :, k, :] = t.reshape(2, P, PLANES[1], WIN).transpose(2, 0, 1, 3)
    return np.ascontiguousarray(planes.reshape(2 * PLANES[1], P, P).transpose(1, 0, 2))


def _node_weights(lin_s, lin_v, sc_s, sc_v):
    to = np.zeros((P, S_ALL + V_ALL), np.float32)
    to[0:S_CH, 0:S_ALL] = np.concatenate([sc_s, lin_s], 1)
    for i in range(3):
        for n, w in enumerate((lin_v, sc_v)):
            to[P - VC + i:P:3, S_ALL + n * VC + i:S_ALL + (n + 1) * VC:3] = w
    return to


def _block_rows(full):
    c = np.zeros((P, 2, full.shape[1]), np.float32)
    c[:, 0] = full[0:P]
    c[0:D - P, 1] = full[P:D]
    return c


def _square(s, v):
    full = np.zeros((D, s.shape[1] + 3 * v.shape[1]), np.float32)
    full[0:S_CH, 0:s.shape[1]] = s
    for i in range(3):
        full[S_CH + i:D:3, s.shape[1] + i::3] = v
    return full


def _ones(value, *shape):
    return np.full(shape, value, np.float32)


def kernel(x, src, dst, edge_attr_4, edge_attr_64, node_vec1, L0_gnn_lin1_ws, L0_gnn_lin1_wv, L0_gnn_fc_w1,
           L0_gnn_fc_w2, L0_gnn_sc_ws, L0_gnn_sc_wv, L0_gnn_lin2_ws, L0_gnn_lin2_wv, L1_gnn_W1, L1_gnn_W2,
           L1_gnn_W3, L1_gnn_W4, L1_gnn_W5, L1_gnn_Ws, L1_gnn_Wv):
    import concourse.bacc as bacc
    from concourse.bass_utils import run_bass_kernel_spmd

    A = lambda v: np.asarray(v)

    def pad(v, n, mode="constant"):
        v = A(v)
        return np.pad(v, [(0, n - v.shape[0])] + [(0, 0)] * (v.ndim - 1), mode=mode)

    by_edge = lambda v: np.ascontiguousarray(np.moveaxis(v.reshape((SLOTS * TILES, P) + v.shape[1:]), 0, 1))
    order = lambda v: np.ascontiguousarray(v.reshape((SLOTS, 2, 2, P) + v.shape[1:]).swapaxes(1, 2).reshape(v.shape))
    e_src = order(pad(src, E_PAD))
    e_dst = order(pad(dst, E_PAD, "edge"))
    e_sh = order(pad(edge_attr_4, E_PAD))
    feat = pad(edge_attr_64, E_PAD).reshape(SLOTS, 2, GROUP // 2, S_CH).transpose(0, 1, 3, 2).reshape(SLOTS, P, GROUP // 2)

    f = float
    i_s, i_v = f(S_CH) ** -0.5, f(V_CH) ** -0.5
    lin_sc = _node_weights(A(L0_gnn_lin1_ws), A(L0_gnn_lin1_wv), A(L0_gnn_sc_ws), A(L0_gnn_sc_wv))
    lin_k = _node_weights(_ones(i_s, S_CH, S_CH), _ones(i_v, V_CH, V_CH), _ones(i_s, S_CH, S_OUT), _ones(i_v, V_CH, V_CH))
    fc1 = np.zeros((P, P), np.float32)
    fc2 = np.zeros((P, 2 * W_N), np.float32)
    for h in range(2):
        fc1[h * 64:(h + 1) * 64, h * 64:(h + 1) * 64] = A(L0_gnn_fc_w1)
        fc2[h * 64:(h + 1) * 64, h * W_N:(h + 1) * W_N] = A(L0_gnn_fc_w2)
    k_s = 64.0 ** -0.5 * 16.0 ** -0.5 * 96.0 ** -0.5
    k_v = 64.0 ** -0.5 * 16.0 ** -0.5 * 128.0 ** -0.5
    ks = np.concatenate([_ones(k_s, 64, 96), _ones(k_s * 3.0 ** -0.5, 32, 96)])
    kv = np.concatenate([_ones(k_v, 96, 32), _ones(k_v * 2.0 ** -0.5, 32, 32)])
    c0, c1 = (S_CH + V_CH) ** -0.5, (3.0 / (S_CH + 2 * V_CH)) ** 0.5
    inv3, inv6 = 3.0 ** -0.5, 6.0 ** -0.5

    arrays = {
        "x": pad(x, NPAD),
        "node_vec": np.ascontiguousarray(pad(node_vec1, NPAD).reshape(NT, P).T),
        "src_idx": np.ascontiguousarray(e_src.reshape(SLOTS // 2, 2 * TILES, P).transpose(0, 2, 1)),
        "dst_idx": by_edge(e_dst),
        "edge_sh": by_edge(e_sh),
        "edge_feat": np.ascontiguousarray(feat),
        "ident": np.eye(P, dtype=np.float32),
        "iota": np.tile(np.arange(WIN, dtype=np.float32), (P, 1)),
        "lin_sc": lin_sc,
        "lin_sc_scale": lin_k,
        "fc1": fc1,
        "fc2": fc2,
        "big0": _layer0_planes(A(L0_gnn_lin2_ws), A(L0_gnn_lin2_wv), False),
        "big0_scale": _layer0_planes(ks, kv, True),
        "l1_pair": _layer1_pair(A(L1_gnn_W1), A(L1_gnn_W2), A(L1_gnn_W3), A(L1_gnn_W4), A(L1_gnn_W5), False),
        "l1_pair_scale": _layer1_pair(_ones(c0, 64, 64), _ones(c0 * inv3, 32, 64), _ones(c1 * inv3, 64, 32),
                                      _ones(c1 * inv3, 32, 32), _ones(c1 * inv6, 32, 32), True),
        "l1_out": _block_rows(_square(A(L1_gnn_Ws), A(L1_gnn_Wv))),
        "l1_out_scale": _block_rows(_square(_ones(i_s, 64, 64), _ones(i_v, 32, 32))),
    }
    nc = bacc.Bacc("TRN2", target_bir_lowering=False, num_devices=1)
    args = [nc.dram_tensor(n + "_dram", v.shape, mybir.dt.from_np(v.dtype), kind="ExternalInput").ap()
            for n, v in arrays.items()]
    out = nc.dram_tensor("out_dram", (NPAD, D), F32, kind="ExternalOutput").ap()
    build(nc, *args, out)
    r = run_bass_kernel_spmd(nc, [{n + "_dram": v for n, v in arrays.items()}], core_ids=[0])
    return r.results[0]["out_dram"][0:N]
```
